# Optimizing a Trainium2 kernel written in Bass

```python
import numpy as np
import jax
import jax.numpy as jnp

def _softmax(x, axis=-1):
    return jax.nn.softmax(x, axis=axis)

def _gelu(x):
    return jax.nn.gelu(x, approximate=True)

def _silu(x):
    return jax.nn.silu(x)

def _sigmoid(x):
    return jax.nn.sigmoid(x)

def _layernorm(x, axis=-1, eps=1e-05):
    m = jnp.mean(x, axis=axis, keepdims=True)
    v = jnp.var(x, axis=axis, keepdims=True)
    return (x - m) / jnp.sqrt(v + eps)

def _scatter_add(tgt, idx, src, axis=0):
    return tgt.at[idx].add(src)

def _segment_sum(src, seg, n):
    return jax.ops.segment_sum(src, seg, n)
kernel_name = 'mk_dlrm_tower_d1_rec_r8_53687d'

def setup_inputs(seed: int=0):
    np.random.seed(seed)
    _w = jnp.asarray

    def _rec_inputs():
        import jax
        import jax.numpy as jnp
        _tk = jax.random.key(seed)
        dense_ctx = jax.random.normal(jax.random.fold_in(_tk, 190), (512, 16), jnp.float32)
        ids = jnp.stack([jax.random.randint(jax.random.fold_in(_tk, 200 + f), (512,), 0, v, jnp.int32) for f, v in enumerate([12500, 12500, 1000, 12500, 1000, 125000, 12500, 1250, 1250, 12500, 1250, 125000, 12500, 1000, 1250, 1250, 1250, 12500, 12500, 125000, 125000, 1000, 12500, 12500, 1000, 1000, 1250, 125000, 1250, 1000, 1250, 1250, 1250, 1250, 1000, 125000, 1000, 1000, 125000])], axis=1)
        tbl_0 = 0.05 * jax.random.normal(jax.random.fold_in(_tk, 500 + 0), (12500, 16), jnp.float32)
        tbl_1 = 0.05 * jax.random.normal(jax.random.fold_in(_tk, 500 + 1), (12500, 16), jnp.float32)
        tbl_2 = 0.05 * jax.random.normal(jax.random.fold_in(_tk, 500 + 2), (1000, 16), jnp.float32)
        tbl_3 = 0.05 * jax.random.normal(jax.random.fold_in(_tk, 500 + 3), (12500, 16), jnp.float32)
        tbl_4 = 0.05 * jax.random.normal(jax.random.fold_in(_tk, 500 + 4), (1000, 16), jnp.float32)
        tbl_5 = 0.05 * jax.random.normal(jax.random.fold_in(_tk, 500 + 5), (125000, 16), jnp.float32)
        tbl_6 = 0.05 * jax.random.normal(jax.random.fold_in(_tk, 500 + 6), (12500, 16), jnp.float32)
        tbl_7 = 0.05 * jax.random.normal(jax.random.fold_in(_tk, 500 + 7), (1250, 16), jnp.float32)
        tbl_8 = 0.05 * jax.random.normal(jax.random.fold_in(_tk, 500 + 8), (1250, 16), jnp.float32)
        tbl_9 = 0.05 * jax.random.normal(jax.random.fold_in(_tk, 500 + 9), (12500, 16), jnp.float32)
        tbl_10 = 0.05 * jax.random.normal(jax.random.fold_in(_tk, 500 + 10), (1250, 16), jnp.float32)
        tbl_11 = 0.05 * jax.random.normal(jax.random.fold_in(_tk, 500 + 11), (125000, 16), jnp.float32)
        tbl_12 = 0.05 * jax.random.normal(jax.random.fold_in(_tk, 500 + 12), (12500, 16), jnp.float32)
        tbl_13 = 0.05 * jax.random.normal(jax.random.fold_in(_tk, 500 + 13), (1000, 16), jnp.float32)
        tbl_14 = 0.05 * jax.random.normal(jax.random.fold_in(_tk, 500 + 14), (1250, 16), jnp.float32)
        tbl_15 = 0.05 * jax.random.normal(jax.random.fold_in(_tk, 500 + 15), (1250, 16), jnp.float32)
        tbl_16 = 0.05 * jax.random.normal(jax.random.fold_in(_tk, 500 + 16), (1250, 16), jnp.float32)
        tbl_17 = 0.05 * jax.random.normal(jax.random.fold_in(_tk, 500 + 17), (12500, 16), jnp.float32)
        tbl_18 = 0.05 * jax.random.normal(jax.random.fold_in(_tk, 500 + 18), (12500, 16), jnp.float32)
        tbl_19 = 0.05 * jax.random.normal(jax.random.fold_in(_tk, 500 + 19), (125000, 16), jnp.float32)
        tbl_20 = 0.05 * jax.random.normal(jax.random.fold_in(_tk, 500 + 20), (125000, 16), jnp.float32)
        tbl_21 = 0.05 * jax.random.normal(jax.random.fold_in(_tk, 500 + 21), (1000, 16), jnp.float32)
        tbl_22 = 0.05 * jax.random.normal(jax.random.fold_in(_tk, 500 + 22), (12500, 16), jnp.float32)
        tbl_23 = 0.05 * jax.random.normal(jax.random.fold_in(_tk, 500 + 23), (12500, 16), jnp.float32)
        tbl_24 = 0.05 * jax.random.normal(jax.random.fold_in(_tk, 500 + 24), (1000, 16), jnp.float32)
        tbl_25 = 0.05 * jax.random.normal(jax.random.fold_in(_tk, 500 + 25), (1000, 16), jnp.float32)
        tbl_26 = 0.05 * jax.random.normal(jax.random.fold_in(_tk, 500 + 26), (1250, 16), jnp.float32)
        tbl_27 = 0.05 * jax.random.normal(jax.random.fold_in(_tk, 500 + 27), (125000, 16), jnp.float32)
        tbl_28 = 0.05 * jax.random.normal(jax.random.fold_in(_tk, 500 + 28), (1250, 16), jnp.float32)
        tbl_29 = 0.05 * jax.random.normal(jax.random.fold_in(_tk, 500 + 29), (1000, 16), jnp.float32)
        tbl_30 = 0.05 * jax.random.normal(jax.random.fold_in(_tk, 500 + 30), (1250, 16), jnp.float32)
        tbl_31 = 0.05 * jax.random.normal(jax.random.fold_in(_tk, 500 + 31), (1250, 16), jnp.float32)
        tbl_32 = 0.05 * jax.random.normal(jax.random.fold_in(_tk, 500 + 32), (1250, 16), jnp.float32)
        tbl_33 = 0.05 * jax.random.normal(jax.random.fold_in(_tk, 500 + 33), (1250, 16), jnp.float32)
        tbl_34 = 0.05 * jax.random.normal(jax.random.fold_in(_tk, 500 + 34), (1000, 16), jnp.float32)
        tbl_35 = 0.05 * jax.random.normal(jax.random.fold_in(_tk, 500 + 35), (125000, 16), jnp.float32)
        tbl_36 = 0.05 * jax.random.normal(jax.random.fold_in(_tk, 500 + 36), (1000, 16), jnp.float32)
        tbl_37 = 0.05 * jax.random.normal(jax.random.fold_in(_tk, 500 + 37), (1000, 16), jnp.float32)
        tbl_38 = 0.05 * jax.random.normal(jax.random.fold_in(_tk, 500 + 38), (125000, 16), jnp.float32)
        _rk = jax.random.fold_in(_tk, 7)
        W_top1 = 0.0693375 * jax.random.normal(jax.random.fold_in(_tk, 801), (208, 512), jnp.float32)
        W_top2 = 0.0441942 * jax.random.normal(jax.random.fold_in(_tk, 802), (512, 256), jnp.float32)
        W_top3 = 0.0625 * jax.random.normal(jax.random.fold_in(_tk, 803), (256, 1), jnp.float32)
        b_top1 = jnp.zeros((512,), jnp.float32)
        b_top2 = jnp.zeros((256,), jnp.float32)
        return (dense_ctx, ids, tbl_0, tbl_1, tbl_2, tbl_3, tbl_4, tbl_5, tbl_6, tbl_7, tbl_8, tbl_9, tbl_10, tbl_11, tbl_12, tbl_13, tbl_14, tbl_15, tbl_16, tbl_17, tbl_18, tbl_19, tbl_20, tbl_21, tbl_22, tbl_23, tbl_24, tbl_25, tbl_26, tbl_27, tbl_28, tbl_29, tbl_30, tbl_31, tbl_32, tbl_33, tbl_34, tbl_35, tbl_36, tbl_37, tbl_38, W_top1, b_top1, W_top2, b_top2, W_top3)
    dense_ctx, ids, tbl_0, tbl_1, tbl_2, tbl_3, tbl_4, tbl_5, tbl_6, tbl_7, tbl_8, tbl_9, tbl_10, tbl_11, tbl_12, tbl_13, tbl_14, tbl_15, tbl_16, tbl_17, tbl_18, tbl_19, tbl_20, tbl_21, tbl_22, tbl_23, tbl_24, tbl_25, tbl_26, tbl_27, tbl_28, tbl_29, tbl_30, tbl_31, tbl_32, tbl_33, tbl_34, tbl_35, tbl_36, tbl_37, tbl_38, W_top1, b_top1, W_top2, b_top2, W_top3 = _rec_inputs()

    def _L0_rec_setup():
        import jax, jax.numpy as jnp
        import numpy as np
        key = jax.random.key(seed)
        k1, k2, k3 = jax.random.split(key, 3)
        B, F0, D = (1024, 39, 16)
        L = 128
        hash_x = jax.random.normal(k1, (B, F0, D), dtype=jnp.float32)
        W0 = jax.random.normal(k2, (F0 * F0, L), dtype=jnp.float32) * 0.05
        W1 = jax.random.normal(k3, (F0 * (L // 2), L), dtype=jnp.float32) * 0.05
        return {'hash_x': hash_x, 'W0': W0, 'W1': W1}
    _L0_rec_all = _L0_rec_setup()
    _L0_rec_in = {k: v for k, v in _L0_rec_all.items() if k in ('W0', 'W1')}
    del _L0_rec_all
    return {'dense_ctx': dense_ctx, 'ids': ids, 'tbl_0': tbl_0, 'tbl_1': tbl_1, 'tbl_2': tbl_2, 'tbl_3': tbl_3, 'tbl_4': tbl_4, 'tbl_5': tbl_5, 'tbl_6': tbl_6, 'tbl_7': tbl_7, 'tbl_8': tbl_8, 'tbl_9': tbl_9, 'tbl_10': tbl_10, 'tbl_11': tbl_11, 'tbl_12': tbl_12, 'tbl_13': tbl_13, 'tbl_14': tbl_14, 'tbl_15': tbl_15, 'tbl_16': tbl_16, 'tbl_17': tbl_17, 'tbl_18': tbl_18, 'tbl_19': tbl_19, 'tbl_20': tbl_20, 'tbl_21': tbl_21, 'tbl_22': tbl_22, 'tbl_23': tbl_23, 'tbl_24': tbl_24, 'tbl_25': tbl_25, 'tbl_26': tbl_26, 'tbl_27': tbl_27, 'tbl_28': tbl_28, 'tbl_29': tbl_29, 'tbl_30': tbl_30, 'tbl_31': tbl_31, 'tbl_32': tbl_32, 'tbl_33': tbl_33, 'tbl_34': tbl_34, 'tbl_35': tbl_35, 'tbl_36': tbl_36, 'tbl_37': tbl_37, 'tbl_38': tbl_38, 'W_top1': W_top1, 'b_top1': b_top1, 'W_top2': W_top2, 'b_top2': b_top2, 'W_top3': W_top3, 'L0_rec_W0': _L0_rec_in['W0'], 'L0_rec_W1': _L0_rec_in['W1']}

def reference(dense_ctx, ids, tbl_0, tbl_1, tbl_2, tbl_3, tbl_4, tbl_5, tbl_6, tbl_7, tbl_8, tbl_9, tbl_10, tbl_11, tbl_12, tbl_13, tbl_14, tbl_15, tbl_16, tbl_17, tbl_18, tbl_19, tbl_20, tbl_21, tbl_22, tbl_23, tbl_24, tbl_25, tbl_26, tbl_27, tbl_28, tbl_29, tbl_30, tbl_31, tbl_32, tbl_33, tbl_34, tbl_35, tbl_36, tbl_37, tbl_38, W_top1, b_top1, W_top2, b_top2, W_top3, L0_rec_W0, L0_rec_W1):
    import jax
    import jax.numpy as jnp

    def _L0_rec_ref(hash_x, W0, W1):
        import jax, jax.numpy as jnp
        import numpy as np
        x0 = hash_x
        B, F0, D = x0.shape
        L = W0.shape[1]
        z0 = jnp.einsum('bid,bjd->bdij', x0, x0).reshape(B, D, F0 * F0)
        cur0 = jax.nn.relu(jnp.einsum('bdk,kl->bld', z0, W0))
        next_h, direct0 = jnp.split(cur0, 2, axis=1)
        Fk = next_h.shape[1]
        z1 = jnp.einsum('bid,bjd->bdij', x0, next_h).reshape(B, D, F0 * Fk)
        cur1 = jax.nn.relu(jnp.einsum('bdk,kl->bld', z1, W1))
        result = jnp.concatenate([direct0, cur1], axis=1)
        return jnp.sum(result, axis=-1)
    e = jnp.stack([tbl_0[ids[:, 0]], tbl_1[ids[:, 1]], tbl_2[ids[:, 2]], tbl_3[ids[:, 3]], tbl_4[ids[:, 4]], tbl_5[ids[:, 5]], tbl_6[ids[:, 6]], tbl_7[ids[:, 7]], tbl_8[ids[:, 8]], tbl_9[ids[:, 9]], tbl_10[ids[:, 10]], tbl_11[ids[:, 11]], tbl_12[ids[:, 12]], tbl_13[ids[:, 13]], tbl_14[ids[:, 14]], tbl_15[ids[:, 15]], tbl_16[ids[:, 16]], tbl_17[ids[:, 17]], tbl_18[ids[:, 18]], tbl_19[ids[:, 19]], tbl_20[ids[:, 20]], tbl_21[ids[:, 21]], tbl_22[ids[:, 22]], tbl_23[ids[:, 23]], tbl_24[ids[:, 24]], tbl_25[ids[:, 25]], tbl_26[ids[:, 26]], tbl_27[ids[:, 27]], tbl_28[ids[:, 28]], tbl_29[ids[:, 29]], tbl_30[ids[:, 30]], tbl_31[ids[:, 31]], tbl_32[ids[:, 32]], tbl_33[ids[:, 33]], tbl_34[ids[:, 34]], tbl_35[ids[:, 35]], tbl_36[ids[:, 36]], tbl_37[ids[:, 37]], tbl_38[ids[:, 38]]], axis=1)
    z = _L0_rec_ref(e, L0_rec_W0, L0_rec_W1)
    z = z.reshape(z.shape[0], -1)
    h = jnp.concatenate([z, dense_ctx], axis=1)
    h = jnp.maximum(h @ W_top1 + b_top1, 0.0)
    h = jnp.maximum(h @ W_top2 + b_top2, 0.0)
    y = h @ W_top3
    return y

_drawn_inputs = setup_inputs


def setup_inputs(seed=0):
    import zlib

    import numpy as np

    out = dict(_drawn_inputs(seed))
    spreads = {'b_top1': (0.0, 0.8), 'b_top2': (0.0, 0.457)}
    factors = {'tbl_0': 8.0,
     'tbl_1': 8.0,
     'tbl_2': 8.0,
     'tbl_3': 8.0,
     'tbl_4': 8.0,
     'tbl_5': 8.0,
     'tbl_6': 8.0,
     'tbl_7': 8.0,
     'tbl_8': 8.0,
     'tbl_9': 8.0,
     'tbl_10': 8.0,
     'tbl_11': 8.0,
     'tbl_12': 8.0,
     'tbl_13': 8.0,
     'tbl_14': 8.0,
     'tbl_15': 8.0,
     'tbl_16': 8.0,
     'tbl_17': 8.0,
     'tbl_18': 8.0,
     'tbl_19': 8.0,
     'tbl_20': 8.0,
     'tbl_21': 8.0,
     'tbl_22': 8.0,
     'tbl_23': 8.0,
     'tbl_24': 8.0,
     'tbl_25': 8.0,
     'tbl_26': 8.0,
     'tbl_27': 8.0,
     'tbl_28': 8.0,
     'tbl_29': 8.0,
     'tbl_30': 8.0,
     'tbl_31': 8.0,
     'tbl_32': 8.0,
     'tbl_33': 8.0,
     'tbl_34': 8.0,
     'tbl_35': 8.0,
     'tbl_36': 8.0,
     'tbl_37': 8.0,
     'tbl_38': 8.0,
     'L0_rec_W1': 8.0}
    for name, (base, spread) in spreads.items():
        noise = np.random.default_rng([zlib.crc32(name.encode()), seed]).standard_normal(out[name].shape)
        drawn = base * np.exp(spread * noise) if base else spread * noise
        out[name] = jnp.asarray(drawn.astype(out[name].dtype))
    for name, factor in factors.items():
        out[name] = (out[name] * factor).astype(out[name].dtype)
    return out
```

```python
from contextlib import ExitStack

import numpy as np

import concourse.bass as bass
from concourse import mybir

ALU = mybir.AluOpType
ACT = mybir.ActivationFunctionType
AX = mybir.AxisListType
F32 = mybir.dt.float32
F32R = mybir.dt.float32r
I32 = mybir.dt.int32
U32 = mybir.dt.uint32

P = 128
B = 512
F = 39
D = 16
HALF = 64
CB = 32
N = CB * D
CHUNKS = B // CB
SETS = 3
GP = SETS * F
SLOTS = -(-CB // SETS)
GW = SLOTS * D
SET_ROWS = [SLOTS, SLOTS, CB - 2 * SLOTS]
OFFSETS = F // 2 + 1
T0 = -(-OFFSETS // SETS)
T1 = -(-F // 2)
TILES = T0 + T1
XR = 2 * F
DENSE = 16
M1, M2 = 512, 256

KINDS0 = "WVWV"
KINDS1 = "PVPVPVPVPV"
GROUPS0 = [[t for t in (2 * g, 2 * g + 1) if t < T0] for g in range(len(KINDS0))]
GROUPS1 = [[T0 + 2 * g, T0 + 2 * g + 1] for g in range(len(KINDS1))]
STEP = len(KINDS1) + len(KINDS0)
RING = 4
PAIRS = 2
SPREAD_AHEAD = 3
MULT_AHEAD = 2


class Spot:

    def __init__(self, layer, chunk, parity, k, index, bases, before):
        self.layer, self.chunk, self.parity, self.k = layer, chunk, parity, k
        self.kind = (KINDS0, KINDS1)[layer][k]
        self.tiles = (GROUPS0, GROUPS1)[layer][k]
        self.last = k == len((KINDS0, KINDS1)[layer]) - 1
        self.ring = index % RING
        self.pair = index % PAIRS
        self.rows = GP if layer == 0 else P
        self.bases, self.upto = bases, before

    def count(self, kinds="WVP"):
        return sum(self.upto[x] for x in kinds) + sum(self.bases[x] for x in kinds)


def segment(groups, bases):
    seen, out = {"W": 0, "V": 0, "P": 0}, []
    for index, (layer, chunk, parity, k) in enumerate(groups):
        seen[(KINDS0, KINDS1)[layer][k]] += 1
        out.append(Spot(layer, chunk, parity, k, index, bases, dict(seen)))
    return out


def layer_groups(layer, chunk, parity):
    return [(layer, chunk, parity, k) for k in range(len((KINDS0, KINDS1)[layer]))]


def prologue():
    return segment(layer_groups(0, 0, 0) + layer_groups(0, 1, 1), {x: 0 for x in "WVP"})


def body(j):
    bases = {x: 2 * KINDS0.count(x) + j * (KINDS0 + KINDS1).count(x) for x in "WVP"}
    return segment(layer_groups(1, j, 0) + layer_groups(0, j + 2, 0)
                   + layer_groups(1, j + 1, 1) + layer_groups(0, j + 3, 1), bases)


def tail():
    bases = {x: 2 * KINDS0.count(x) + (CHUNKS - 2) * (KINDS0 + KINDS1).count(x) for x in "WVP"}
    return segment(layer_groups(1, CHUNKS - 2, 0) + layer_groups(1, CHUNKS - 1, 1), bases)


def last_of_layer0(chunk):
    return 2 * len(KINDS0) + (chunk - 1) * STEP


def build(nc, ids, base, table, select, w0a, w0b, w1, wt1, bt1, wt2, bt2, wt3, dense, out):
    assert (2 * len(KINDS0)) % RING == 0 and (2 * STEP) % RING == 0
    with ExitStack() as ctx:
        def sb(name, shape, dt=F32):
            return ctx.enter_context(nc.sbuf_tensor(name, shape, dt))

        def sem(name):
            return ctx.enter_context(nc.semaphore(name))

        ids_sb = sb("ids_sb", [GP, CHUNKS * SLOTS], I32)
        base_sb = sb("base_sb", [GP, 1])
        rows_sb = sb("rows_sb", [GP, CHUNKS * SLOTS], U32)
        rows_now = sb("rows_now", [GP, 2, SLOTS], U32)
        found = sb("found", [GP, 2, GW])
        part_hi = sb("part_hi", [GP, 2, GW], F32R)
        part_lo = sb("part_lo", [GP, 2, GW], F32R)
        x_parts = sb("x_parts", [XR, CHUNKS * N], F32R)
        x_three = sb("x_three", [GP, 2, N])
        select_in = sb("select_in", [XR, TILES * P])
        select_sb = sb("select_sb", [XR, TILES, P], F32R)
        w_sum = sb("w_sum", [P, TILES, P])
        w0b_sb = sb("w0b_sb", [GP, T0, P])
        w_hi = sb("w_hi", [P, TILES, P], F32R)
        w_lo = sb("w_lo", [P, TILES, P], F32R)
        z = sb("z", [P, RING, 2, N])
        z_hi = sb("z_hi", [P, RING, 2, N], F32R)
        z_lo = sb("z_lo", [P, RING, 2, N], F32R)
        h = sb("h", [P, 2, N])
        direct = sb("direct", [HALF, N])
        cur1 = sb("cur1", [P, N])
        feat_a = sb("feat_a", [P, B])
        feat_b = sb("feat_b", [HALF + DENSE, B])
        wt1a_sb = sb("wt1a_sb", [P, M1])
        wt1b_sb = sb("wt1b_sb", [HALF + DENSE, M1])
        wt2_sb = sb("wt2_sb", [P, M1 // P, M2])
        wt3_sb = sb("wt3_sb", [P, M2 // P])
        bt1_sb = sb("bt1_sb", [P, M1 // P])
        bt2_sb = sb("bt2_sb", [P, M2 // P])
        y_sb = sb("y_sb", [1, B])

        spread = ctx.enter_context(nc.psum_tensor("spread", [P, PAIRS, 2, N], F32))
        acc0 = ctx.enter_context(nc.psum_tensor("acc0", [P, 2, N], F32))
        acc1 = ctx.enter_context(nc.psum_tensor("acc1", [P, N], F32))
        acc_y = ctx.enter_context(nc.psum_tensor("acc_y", [P, N], F32))

        hid1 = [z[:, m // 2, m % 2, :] for m in range(M1 // P)]
        hid2 = [z[:, 2, m, :] for m in range(M2 // P)]
        hid1_acc = [spread[:, m // 2, m % 2, :] for m in range(M1 // P)]
        hid2_acc = [acc0[:, m, :] for m in range(M2 // P)]

        ids_in = sem("ids_in")
        select_in_done = sem("select_in_done")
        w0_in = sem("w0_in")
        w1_in = sem("w1_in")
        mlp_in = sem("mlp_in")
        rows_ready = sem("rows_ready")
        rows_placed = sem("rows_placed")
        select_ready = sem("select_ready")
        wsum_ready = sem("wsum_ready")
        whi_ready = sem("whi_ready")
        wlo_ready = sem("wlo_ready")
        gathered = [sem("gathered_even"), sem("gathered_odd")]
        xsplit = sem("xsplit")
        parts_in = [sem("parts_even"), sem("parts_odd")]
        three_in = [sem("three_even"), sem("three_odd")]
        spread_done = sem("spread_done")
        mult_done = sem("mult_done")
        hi_done = sem("hi_done")
        lo_done = {"V": sem("lo_done_vector"), "P": sem("lo_done_pool")}
        contracted = sem("contracted")
        h_ready = sem("h_ready")
        evicted = sem("evicted")
        reduced = sem("reduced")
        hid1_done = sem("hid1_done")
        hid1_relu = sem("hid1_relu")
        hid2_done = sem("hid2_done")
        hid2_relu = sem("hid2_relu")
        y_done = sem("y_done")
        y_ready = sem("y_ready")
        out_done = sem("out_done")

        n_parts, n_three = 2 * SETS, SETS * SETS

        def dma_total(chunk, parity, per_chunk):
            return 8 * per_chunk * (chunk - parity) + 16 * per_chunk

        def columns(chunk):
            return bass.ds(chunk * N, N)

        block = ctx.enter_context(nc.Block())

        @block.sync
        def _(sp):
            sp.dma_start(ids_sb[:, :], ids).then_inc(ids_in, 16)
            sp.dma_start(base_sb[:, :], base).then_inc(ids_in, 16)
            sp.dma_start(select_in[:, :], select).then_inc(select_in_done, 16)
            sp.dma_start(w_sum[:, T0:, :], w1).then_inc(w1_in, 16)
            for dst, src in ((wt1a_sb[:, :], wt1[HALF:HALF + P, :]),
                             (wt1b_sb[0:HALF, :], wt1[0:HALF, :]),
                             (wt1b_sb[HALF:, :], wt1[HALF + P:, :]),
                             (wt2_sb[:, :, :], wt2), (wt3_sb[:, :], wt3), (bt1_sb[:, :], bt1),
                             (bt2_sb[:, :], bt2), (feat_b[HALF:, :], dense)):
                sp.dma_start(dst, src).then_inc(mlp_in, 16)

            def lay_out(chunk, par):
                sp.wait_ge(xsplit, 2 * chunk + 2)
                for s in range(SETS):
                    w = SET_ROWS[s] * D
                    for part, src in enumerate((part_hi, part_lo)):
                        sp.dma_start(x_parts[F * part:F * part + F, bass.ds(chunk * N + s * GW, w)].bitcast(F32),
                                     src[F * s:F * s + F, par, 0:w].bitcast(F32)).then_inc(parts_in[par], 16)
                    for copy in range(SETS):
                        sp.dma_start(x_three[F * copy:F * copy + F, par, s * GW:s * GW + w],
                                     found[F * s:F * s + F, par, 0:w]).then_inc(three_in[par], 16)

            lay_out(0, 0)
            lay_out(1, 1)
            with sp.Fori(0, CHUNKS - 3, 2) as j:
                for par in (0, 1):
                    if par == 0:
                        sp.wait_ge(mult_done, len(KINDS0) + j * STEP)
                    else:
                        sp.wait_ge(mult_done, 2 * len(KINDS0) + j * STEP)
                    lay_out(j + 2 + par, par)
            sp.wait_ge(y_ready, 1)
            sp.dma_start(out, y_sb[:, :]).then_inc(out_done, 16)
            sp.wait_ge(out_done, 16)

        @block.gpsimd
        def _(pool):
            def place_rows(chunk, par):
                nc.gpsimd.tensor_copy(rows_now[:, par, :],
                                      rows_sb[:, bass.ds(chunk * SLOTS, SLOTS)]).then_inc(rows_placed, 1)
                pool.wait_ge(rows_placed, chunk + 1)
                pool.nop(nofuse=True)

            def gather(par, slots):
                for s in slots:
                    pool.indirect_dma_start(
                        out=found[:, par, s * D:s * D + D], out_offset=None, in_=table,
                        in_offset=bass.IndirectOffsetOnAxis(ap=rows_now[:, par, s:s + 1], axis=0)
                    ).then_inc(gathered[par], 16)

            def low_part(spot):
                r, n = spot.rows, len(spot.tiles)
                pool.wait_ge(hi_done, spot.count("VP"))
                nc.gpsimd.tensor_tensor(z_lo[0:r, spot.ring, 0:n], z[0:r, spot.ring, 0:n],
                                        z_hi[0:r, spot.ring, 0:n], ALU.subtract).then_inc(lo_done["P"], 1)

            pool.wait_ge(rows_ready, 1)
            place_rows(0, 0)
            gather(0, range(SLOTS))
            place_rows(1, 1)
            gather(1, range(SLOTS))
            pool.wait_ge(xsplit, 2)
            pool.wait_ge(three_in[0], 16 * n_three)
            place_rows(2, 0)
            gather(0, range(SLOTS))
            with pool.Fori(0, CHUNKS - 5, 2) as j:
                for n, spot in enumerate(body(j)):
                    at, nxt = n % STEP, j + n // STEP + 3
                    par = 1 - n // STEP
                    if spot.kind == "P":
                        low_part(spot)
                    if at == 0:
                        pool.wait_ge(xsplit, 2 * (nxt - 2) + 2)
                        pool.wait_ge(three_in[par], dma_total(nxt - 2, par, n_three))
                        place_rows(nxt, par)
                    gather(par, [s for s in range(SLOTS) if s * STEP // SLOTS == at])
            for n, spot in enumerate(body(CHUNKS - 4) + tail()):
                if spot.kind == "P":
                    low_part(spot)
                if n == 0:
                    pool.wait_ge(xsplit, 2 * (CHUNKS - 3) + 2)
                    pool.wait_ge(three_in[1], dma_total(CHUNKS - 3, 1, n_three))
                    place_rows(CHUNKS - 1, 1)
                    gather(1, range(SLOTS))

        @block.scalar
        def _(act):
            act.dma_start(w_sum[0:GP, 0:T0, :], w0a).then_inc(w0_in, 16)
            act.dma_start(w0b_sb[:, :, :], w0b).then_inc(w0_in, 16)
            act.wait_ge(select_in_done, 16)
            nc.scalar.activation(select_sb[:, :, :].rearrange("p t m -> p (t m)"), select_in[:, :],
                                 ACT.Copy).then_inc(select_ready, 1)
            act.wait_ge(wsum_ready, 1)
            nc.scalar.activation(w_hi[0:GP, 0:T0, :], w_sum[0:GP, 0:T0, :], ACT.Copy).then_inc(whi_ready, 1)
            act.wait_ge(w1_in, 16)
            nc.scalar.activation(w_hi[:, T0:, :], w_sum[:, T0:, :], ACT.Copy).then_inc(whi_ready, 1)

            def high_part(spot):
                act.wait_ge(mult_done, spot.count())
                r, n = spot.rows, len(spot.tiles)
                nc.scalar.activation(z_hi[0:r, spot.ring, 0:n], z[0:r, spot.ring, 0:n],
                                     ACT.Copy).then_inc(hi_done, 1)

            def evict0(chunk, par, groups_done, reduced_before):
                act.wait_ge(contracted, groups_done)
                nc.scalar.activation(h[0:HALF, par, :], acc0[0:HALF, par, :], ACT.Relu).then_inc(h_ready, 1)
                nc.scalar.activation(h[HALF:P, par, :], acc0[0:HALF, par, :], ACT.Relu).then_inc(h_ready, 1)
                if reduced_before is not None:
                    act.wait_ge(reduced, reduced_before)
                nc.scalar.activation(direct[:, :], acc0[HALF:P, par, :], ACT.Relu).then_inc(evicted, 1)

            def evict1(j, groups_done):
                act.wait_ge(contracted, groups_done)
                act.wait_ge(reduced, 2 * j + 1)
                nc.scalar.activation(cur1[:, :], acc1[:, :], ACT.Relu).then_inc(evicted, 1)

            for spot in prologue():
                if spot.kind in "VP":
                    high_part(spot)
                if spot.chunk == 1 and spot.k == 2:
                    evict0(0, 0, spot.count() - 3, None)
            with act.Fori(0, CHUNKS - 3, 2) as j:
                for spot in body(j):
                    if spot.kind in "VP":
                        high_part(spot)
                    if spot.layer == 1 and spot.k == 2:
                        evict0(spot.chunk + 1, 1 - spot.parity, spot.count() - 3, 2 * spot.chunk + 1)
                    if spot.layer == 0 and spot.k == 2:
                        evict1(spot.chunk - 2, spot.count() - 3)
            for spot in tail():
                if spot.kind in "VP":
                    high_part(spot)
                if spot.k == 2 and spot.chunk == CHUNKS - 2:
                    evict0(CHUNKS - 1, 1, spot.count() - 3, 2 * spot.chunk + 1)
                if spot.k == 2 and spot.chunk == CHUNKS - 1:
                    evict1(CHUNKS - 2, spot.count() - 3)
            evict1(CHUNKS - 1, spot.count())

            act.wait_ge(mlp_in, 16 * 8)
            for m in range(M1 // P):
                act.wait_ge(hid1_done, m + 1)
                nc.scalar.activation(hid1[m], hid1_acc[m], ACT.Relu, bias=bt1_sb[:, m:m + 1]).then_inc(hid1_relu, 1)
            for m in range(M2 // P):
                act.wait_ge(hid2_done, m + 1)
                nc.scalar.activation(hid2[m], hid2_acc[m], ACT.Relu, bias=bt2_sb[:, m:m + 1]).then_inc(hid2_relu, 1)
            act.wait_ge(y_done, 1)
            nc.scalar.activation(y_sb[:, :], acc_y[0:1, :], ACT.Copy).then_inc(y_ready, 1)

        @block.vector
        def _(dve):
            def split(chunk, par, part):
                if part == 0:
                    dve.wait_ge(gathered[par], dma_total(chunk, par, SLOTS))
                    nc.vector.tensor_copy(part_hi[:, par, :], found[:, par, :]).then_inc(xsplit, 1)
                else:
                    dve.wait_ge(xsplit, 2 * chunk + 1)
                    nc.vector.tensor_tensor(part_lo[:, par, :], found[:, par, :], part_hi[:, par, :],
                                            ALU.subtract).then_inc(xsplit, 1)

            def multiply(spot, reuses=True):
                r, n = spot.rows, len(spot.tiles)
                if spot.k == 0 and spot.layer == 0:
                    dve.wait_ge(three_in[spot.parity], dma_total(spot.chunk, spot.parity, n_three))
                if spot.k == 0 and spot.layer == 1:
                    dve.wait_ge(h_ready, 2 * spot.chunk + 2)
                if reuses:
                    dve.wait_ge(contracted, spot.count() - RING)
                dve.wait_ge(spread_done, spot.count())
                with_ = x_three[:, spot.parity, :] if spot.layer == 0 else h[:, spot.parity, :]
                nc.vector.tensor_tensor(z[0:r, spot.ring, 0:n], spread[0:r, spot.pair, 0:n],
                                        spread_rows(with_, n), ALU.mult).then_inc(mult_done, 1)

            def spread_rows(ap, n):
                return ap.unsqueeze(1).to_broadcast([ap.shape[0], n, N])

            def low_part(spot):
                r, n = spot.rows, len(spot.tiles)
                dve.wait_ge(hi_done, spot.count("VP"))
                nc.vector.tensor_tensor(z_lo[0:r, spot.ring, 0:n], z[0:r, spot.ring, 0:n],
                                        z_hi[0:r, spot.ring, 0:n], ALU.subtract).then_inc(lo_done["V"], 1)

            def reduce0(chunk, item):
                dve.wait_ge(evicted, item)
                nc.vector.tensor_reduce(feat_b[0:HALF, bass.ds(chunk * CB, CB)],
                                        direct[:, :].rearrange("p (b d) -> p b d", d=D), AX.X,
                                        ALU.add).then_inc(reduced, 1)

            def reduce1(chunk, item):
                dve.wait_ge(evicted, item)
                nc.vector.tensor_reduce(feat_a[:, bass.ds(chunk * CB, CB)],
                                        cur1[:, :].rearrange("p (b d) -> p b d", d=D), AX.X,
                                        ALU.add).then_inc(reduced, 1)

            dve.wait_ge(ids_in, 32)
            nc.vector.tensor_scalar(rows_sb[:, :], ids_sb[:, :], base_sb[:, 0:1], None,
                                    ALU.add).then_inc(rows_ready, 1)
            dve.wait_ge(w0_in, 32)
            nc.vector.tensor_tensor(w_sum[0:GP, 0:T0, :], w_sum[0:GP, 0:T0, :], w0b_sb[:, :, :],
                                    ALU.add).then_inc(wsum_ready, 1)
            for n, (r, t) in enumerate(((GP, slice(0, T0)), (P, slice(T0, TILES)))):
                dve.wait_ge(whi_ready, n + 1)
                nc.vector.tensor_tensor(w_lo[0:r, t, :], w_sum[0:r, t, :], w_hi[0:r, t, :],
                                        ALU.subtract).then_inc(wlo_ready, 1)

            split(0, 0, 0)
            split(0, 0, 1)
            first, start = prologue(), body(0)
            for spot in first[:MULT_AHEAD]:
                multiply(spot, reuses=False)
            for n, spot in enumerate(first):
                if n + MULT_AHEAD == len(KINDS0):
                    split(1, 1, 0)
                    split(1, 1, 1)
                multiply((first + start)[n + MULT_AHEAD], reuses=n + MULT_AHEAD >= RING)
                if spot.kind == "V":
                    low_part(spot)
            reduce0(0, 1)
            with dve.Fori(0, CHUNKS - 3, 2) as j:
                spots, after = body(j), body(j + 2)
                for n, spot in enumerate(spots):
                    multiply((spots + after)[n + MULT_AHEAD])
                    if spot.kind == "V":
                        low_part(spot)
                    step = j + n // STEP
                    if n % STEP in (1, 2):
                        split(step + 2, n // STEP, n % STEP - 1)
                    if n % STEP == 5:
                        reduce0(step + 1, 2 * step + 2)
                    if n % STEP == STEP - 1:
                        reduce1(step, 2 * step + 3)
            last = tail()
            for n, spot in enumerate(last):
                if n + MULT_AHEAD < len(last):
                    multiply(last[n + MULT_AHEAD])
                if spot.kind == "V":
                    low_part(spot)
                if n == 5:
                    reduce0(CHUNKS - 1, 2 * CHUNKS - 2)
                if n == len(KINDS1) + 5:
                    reduce1(CHUNKS - 2, 2 * CHUNKS - 1)
            reduce1(CHUNKS - 1, 2 * CHUNKS)

        @block.tensor
        def _(pe):
            def spread_x(spot, reuses=True):
                if spot.k == 0 and spot.layer == 0:
                    pe.wait_ge(parts_in[spot.parity], dma_total(spot.chunk, spot.parity, n_parts))
                if reuses:
                    pe.wait_ge(mult_done, spot.count() - PAIRS)
                for a, t in enumerate(spot.tiles):
                    last = nc.tensor.matmul(spread[0:spot.rows, spot.pair, a, :], select_sb[:, t, 0:spot.rows],
                                            x_parts[:, columns(spot.chunk)], start=True, stop=True)
                last.then_inc(spread_done, 1)

            def contract(spot, reuses=True):
                r = spot.rows
                acc = acc1[:, :] if spot.layer else acc0[:, spot.parity, :]
                if spot.k == 0 and reuses:
                    pe.wait_ge(evicted, 2 * spot.chunk + 1 if spot.layer else 2 * spot.chunk - 2)
                if spot.kind == "W":
                    pe.wait_ge(mult_done, spot.count())
                    passes = [(w_sum, z, a) for a in range(len(spot.tiles))]
                else:
                    pe.wait_ge(hi_done, spot.count("VP"))
                    passes = [(w, z_hi, a) for a in range(len(spot.tiles)) for w in (w_hi, w_lo)]
                    passes += [(w_hi, z_lo, a) for a in range(len(spot.tiles))]
                for n, (w, of, a) in enumerate(passes):
                    if of is z_lo and a == 0:
                        pe.wait_ge(lo_done[spot.kind], spot.count(spot.kind))
                    last = nc.tensor.matmul(acc, w[0:r, spot.tiles[a], :], of[0:r, spot.ring, a, :],
                                            start=(spot.k == 0 and n == 0),
                                            stop=(spot.last and n == len(passes) - 1))
                last.then_inc(contracted, 1)

            pe.wait_ge(select_ready, 1)
            first, start = prologue(), body(0)
            for n, spot in enumerate(first[:SPREAD_AHEAD]):
                spread_x(spot, reuses=n >= PAIRS)
            pe.wait_ge(wlo_ready, 2)
            for n, spot in enumerate(first):
                spread_x((first + start)[n + SPREAD_AHEAD])
                contract(spot, reuses=False)
            with pe.Fori(0, CHUNKS - 3, 2) as j:
                spots, after = body(j), body(j + 2)
                for n, spot in enumerate(spots):
                    spread_x((spots + after)[n + SPREAD_AHEAD])
                    contract(spot)
            last = tail()
            for n, spot in enumerate(last):
                if n + SPREAD_AHEAD < len(last):
                    spread_x(last[n + SPREAD_AHEAD])
                contract(spot)

            pe.wait_ge(mlp_in, 16 * 8)
            pe.wait_ge(reduced, 2 * CHUNKS)
            for m in range(M1 // P):
                cols = slice(m * P, m * P + P)
                nc.tensor.matmul(hid1_acc[m], wt1b_sb[:, cols], feat_b[:, :], start=True, stop=False)
                nc.tensor.matmul(hid1_acc[m], wt1a_sb[:, cols], feat_a[:, :], start=False,
                                 stop=True).then_inc(hid1_done, 1)
            for m in range(M2 // P):
                for k in range(M1 // P):
                    if m == 0:
                        pe.wait_ge(hid1_relu, k + 1)
                    last = nc.tensor.matmul(hid2_acc[m], wt2_sb[:, k, m * P:m * P + P], hid1[k],
                                            start=(k == 0), stop=(k == M1 // P - 1))
                last.then_inc(hid2_done, 1)
            for k in range(M2 // P):
                pe.wait_ge(hid2_relu, k + 1)
                last = nc.tensor.matmul(acc_y[0:1, :], wt3_sb[:, k:k + 1], hid2[k],
                                        start=(k == 0), stop=(k == M2 // P - 1))
            last.then_inc(y_done, 1)


def layout(inputs):
    ids = np.ascontiguousarray(inputs["ids"]).astype(np.int32)
    tables = [np.ascontiguousarray(inputs[f"tbl_{f}"]) for f in range(F)]
    by_set = np.zeros((SETS, F, CHUNKS, SLOTS), np.int32)
    for s in range(SETS):
        w = SET_ROWS[s]
        rows = ids.reshape(CHUNKS, CB, F)[:, s * SLOTS:s * SLOTS + w]
        by_set[s, :, :, 0:w] = rows.transpose(2, 0, 1)
    starts = np.cumsum([0] + [t.shape[0] for t in tables])[:F].astype(np.float32)

    w0 = np.asarray(inputs["L0_rec_W0"]).reshape(F, F, P)
    w0a, w0b = np.zeros((2, GP, T0, P), np.float32)
    select = np.zeros((XR, TILES, P), np.float32)
    i = np.arange(F)
    for o in range(OFFSETS):
        t, a = divmod(o, SETS)
        j = (i + o) % F
        w0a[F * a + i, t] = w0[i, j]
        if o:
            w0b[F * a + i, t] = w0[j, i]
        for part in range(2):
            select[F * part + j, t, F * a + i] = 1.0
    w1 = np.zeros((T1 * 2, HALF, P), np.float32)
    w1[0:F] = np.asarray(inputs["L0_rec_W1"]).reshape(F, HALF, P)
    for n in range(F):
        for part in range(2):
            select[F * part + n, T0 + n // 2, HALF * (n % 2):HALF * (n % 2) + HALF] = 1.0
    return {
        "ids": by_set.reshape(GP, CHUNKS * SLOTS),
        "base": np.tile(starts, SETS).reshape(GP, 1),
        "table": np.concatenate(tables),
        "select": select.reshape(XR, TILES * P),
        "w0a": w0a,
        "w0b": w0b,
        "w1": np.ascontiguousarray(w1.reshape(T1, P, P).transpose(1, 0, 2)),
        "wt1": np.asarray(inputs["W_top1"]),
        "bt1": np.ascontiguousarray(np.asarray(inputs["b_top1"]).reshape(M1 // P, P).T),
        "wt2": np.ascontiguousarray(np.asarray(inputs["W_top2"]).reshape(M1 // P, P, M2).transpose(1, 0, 2)),
        "bt2": np.ascontiguousarray(np.asarray(inputs["b_top2"]).reshape(M2 // P, P).T),
        "wt3": np.ascontiguousarray(np.asarray(inputs["W_top3"]).reshape(M2 // P, P).T),
        "dense": np.ascontiguousarray(np.asarray(inputs["dense_ctx"]).T),
    }


def kernel(**inputs):
    import concourse.bacc as bacc
    from concourse.bass_utils import run_bass_kernel_spmd

    nc = bacc.Bacc("TRN2", target_bir_lowering=False, num_devices=1)
    arrays, args = {}, []
    for name, a in layout(inputs).items():
        arrays[f"in_{name}_dram"] = a
        args.append(nc.dram_tensor(f"in_{name}_dram", a.shape, mybir.dt.from_np(a.dtype), kind="ExternalInput").ap())
    args.append(nc.dram_tensor("out_0_dram", (1, B), F32, kind="ExternalOutput").ap())
    build(nc, *args)
    got = run_bass_kernel_spmd(nc, [arrays], core_ids=[0]).results[0]["out_0_dram"]
    return got.reshape(B, 1)
```

```python
from contextlib import ExitStack

import numpy as np

import concourse.bass as bass
from concourse import mybir

ALU = mybir.AluOpType
ACT = mybir.ActivationFunctionType
AX = mybir.AxisListType
F32 = mybir.dt.float32
F32R = mybir.dt.float32r
I32 = mybir.dt.int32
U32 = mybir.dt.uint32

P = 128
B = 512
F = 39
D = 16
HALF = 64
CB = 32
N = CB * D
CHUNKS = B // CB
SETS = 3
GP = SETS * F
SLOTS = -(-CB // SETS)
GW = SLOTS * D
SET_ROWS = [SLOTS, SLOTS, CB - 2 * SLOTS]
OFFSETS = F // 2 + 1
T0 = -(-OFFSETS // SETS)
T1 = -(-F // 2)
TILES = T0 + T1
LO = 64
XR = LO + F
DENSE = 16
M1, M2 = 512, 256

KINDS0 = "VWVW"
KINDS1 = "WPVPVPVPVPW"
GROUPS0 = [[t for t in (2 * g, 2 * g + 1) if t < T0] for g in range(len(KINDS0))]
GROUPS1 = [[T0 + 2 * g, T0 + 2 * g + 1] for g in range(len(KINDS1) - 2)] + [[TILES - 2], [TILES - 1]]
STEP = len(KINDS1) + len(KINDS0)
RING = 6
PAIRS = 3
SPREAD_AHEAD = 5
GATHER_AT = [s * STEP // SLOTS for s in range(SLOTS)]
TURN = 4
EVICT1_AT = 2
EVICT0_AT = 5
REDUCE1_AT = 2
REDUCE0_AT = 6
HI_AT = 4
LO_AT = 4
MULT_AHEAD = 3


class Spot:

    def __init__(self, layer, chunk, parity, k, index, bases, before):
        self.layer, self.chunk, self.parity, self.k = layer, chunk, parity, k
        self.kind = (KINDS0, KINDS1)[layer][k]
        self.tiles = (GROUPS0, GROUPS1)[layer][k]
        self.last = k == len((KINDS0, KINDS1)[layer]) - 1
        self.ring = index % RING
        self.pair = index % PAIRS
        self.rows = GP if layer == 0 else P
        self.first = isinstance(chunk, int) and chunk == 0
        self.late = isinstance(chunk, int) and chunk >= CHUNKS - 2
        self.final = isinstance(chunk, int) and chunk == CHUNKS - 1
        self.bases, self.upto = bases, before

    def count(self, kinds="WVP"):
        return sum(self.upto[x] for x in kinds) + sum(self.bases[x] for x in kinds)


def segment(groups, bases, start):
    seen, out = {"W": 0, "V": 0, "P": 0}, []
    for index, (layer, chunk, parity, k) in enumerate(groups, start):
        seen[(KINDS0, KINDS1)[layer][k]] += 1
        out.append(Spot(layer, chunk, parity, k, index, bases, dict(seen)))
    return out


def layer_groups(layer, chunk, parity):
    return [(layer, chunk, parity, k) for k in range(len((KINDS0, KINDS1)[layer]))]


def prologue():
    return segment(layer_groups(0, 0, 0) + layer_groups(0, 1, 1), {x: 0 for x in "WVP"}, 0)


def body(j):
    bases = {x: 2 * KINDS0.count(x) + j * (KINDS0 + KINDS1).count(x) for x in "WVP"}
    return segment(layer_groups(1, j, 0) + layer_groups(0, j + 2, 0)
                   + layer_groups(1, j + 1, 1) + layer_groups(0, j + 3, 1), bases, 2 * len(KINDS0))


def tail():
    bases = {x: 2 * KINDS0.count(x) + (CHUNKS - 2) * (KINDS0 + KINDS1).count(x) for x in "WVP"}
    return segment(layer_groups(1, CHUNKS - 2, 0) + layer_groups(1, CHUNKS - 1, 1), bases, 2 * len(KINDS0))


def head():
    return prologue() + body(0)[:TURN]


def turn(j):
    return body(j)[TURN:] + body(j + 2)[:TURN]


def rest():
    return tail()[TURN:]


def build(nc, ids, base, table, select, w0a, w0b, w1, wt1, bt1, wt2, bt2, wt3, dense, out):
    assert (2 * STEP) % RING == 0 and (2 * STEP) % PAIRS == 0
    with ExitStack() as ctx:
        def sb(name, shape, dt=F32):
            return ctx.enter_context(nc.sbuf_tensor(name, shape, dt))

        def sem(name):
            return ctx.enter_context(nc.semaphore(name))

        ids_sb = sb("ids_sb", [GP, CHUNKS * SLOTS], I32)
        base_sb = sb("base_sb", [GP, 1])
        rows_sb = sb("rows_sb", [GP, CHUNKS * SLOTS], U32)
        rows_now = sb("rows_now", [GP, 2, SLOTS], U32)
        found = sb("found", [GP, 2, GW])
        x_parts = sb("x_parts", [XR, CHUNKS * N], F32R)
        x_three = sb("x_three", [GP, 2, N])
        select_sb = sb("select_sb", [XR, TILES, P], F32R)
        w_sum = sb("w_sum", [P, TILES, P])
        w_hi = sb("w_hi", [P, TILES, P], F32R)
        w_lo = sb("w_lo", [P, TILES, P], F32R)
        z = sb("z", [P, RING, 2, N])
        staging = z[:, :, :, :].rearrange("p r a n -> p (r a n)")
        select_in = staging[0:XR, 0:TILES * P]
        w0b_sb = staging[0:GP, TILES * P:(TILES + T0) * P].rearrange("p (t m) -> p t m", m=P)
        z_hi = sb("z_hi", [P, RING, 2, N], F32R)
        z_lo = sb("z_lo", [P, RING, 2, N], F32R)
        h = sb("h", [P, 2, N])
        direct = sb("direct", [HALF, N])
        cur1 = sb("cur1", [P, N])
        feat_a = sb("feat_a", [P, B])
        feat_b = sb("feat_b", [HALF + DENSE, B])
        wt1a_sb = sb("wt1a_sb", [P, M1])
        wt1b_sb = sb("wt1b_sb", [HALF + DENSE, M1])
        wt2_sb = sb("wt2_sb", [P, M1 // P, M2])
        wt3_sb = sb("wt3_sb", [P, M2 // P])
        bt1_sb = sb("bt1_sb", [P, M1 // P])
        bt2_sb = sb("bt2_sb", [P, M2 // P])
        y_sb = sb("y_sb", [1, B])

        spread = ctx.enter_context(nc.psum_tensor("spread", [P, PAIRS, 2, N], F32))
        acc0 = ctx.enter_context(nc.psum_tensor("acc0", [P, N], F32))
        acc1 = ctx.enter_context(nc.psum_tensor("acc1", [P, N], F32))

        hid1 = [z[:, m // 2, m % 2, :] for m in range(M1 // P)]
        hid2 = [z[:, 2, m, :] for m in range(M2 // P)]
        hid1_acc = [spread[:, m // 2, m % 2, :] for m in range(M1 // P)]
        hid2_acc = [spread[:, 2, m, :] for m in range(M2 // P)]

        ids_in = sem("ids_in")
        select_in_done = sem("select_in_done")
        w0_in = sem("w0_in")
        w1_in = sem("w1_in")
        mlp_in = sem("mlp_in")
        rows_ready = sem("rows_ready")
        rows_placed = sem("rows_placed")
        select_ready = sem("select_ready")
        wsum_ready = sem("wsum_ready")
        whi_ready = sem("whi_ready")
        wlo_ready = sem("wlo_ready")
        gathered = [sem("gathered_even"), sem("gathered_odd")]
        gap_cleared = sem("gap_cleared")
        x_hi_done = sem("x_hi_done")
        x_lo_done = sem("x_lo_done")
        flat_in = [sem("flat_even"), sem("flat_odd")]
        three_in = [sem("three_even"), sem("three_odd")]
        spread_done = sem("spread_done")
        mult_done = sem("mult_done")
        hi_done = sem("hi_done")
        lo_done = {"V": sem("lo_done_vector"), "P": sem("lo_done_pool")}
        contracted = sem("contracted")
        h_ready = sem("h_ready")
        evicted = sem("evicted")
        reduced = sem("reduced")
        hid1_done = sem("hid1_done")
        hid1_relu = sem("hid1_relu")
        hid2_done = sem("hid2_done")
        hid2_relu = sem("hid2_relu")
        y_done = sem("y_done")
        y_ready = sem("y_ready")
        out_done = sem("out_done")

        n_flat, n_three = SETS, SETS - 1

        def dma_total(chunk, parity, per_chunk):
            return 8 * per_chunk * (chunk - parity) + 16 * per_chunk

        def columns(chunk):
            return bass.ds(chunk * N, N)

        block = ctx.enter_context(nc.Block())

        @block.sync
        def _(sp):
            sp.dma_start(ids_sb[:, :], ids).then_inc(ids_in, 16)
            sp.dma_start(base_sb[:, :], base).then_inc(ids_in, 16)
            sp.dma_start(select_in, select).then_inc(select_in_done, 16)
            sp.dma_start(w_sum[:, T0:, :], w1).then_inc(w1_in, 16)
            for dst, src in ((wt1a_sb[:, :], wt1[HALF:HALF + P, :]),
                             (wt1b_sb[0:HALF, :], wt1[0:HALF, :]),
                             (wt1b_sb[HALF:, :], wt1[HALF + P:, :]),
                             (wt2_sb[:, :, :], wt2), (wt3_sb[:, :], wt3), (bt1_sb[:, :], bt1),
                             (bt2_sb[:, :], bt2), (feat_b[HALF:, :], dense)):
                sp.dma_start(dst, src).then_inc(mlp_in, 16)

            def lay_out(chunk, par):
                sp.wait_ge(gathered[par], dma_total(chunk, par, SLOTS))
                for s in range(SETS):
                    w = SET_ROWS[s] * D
                    sp.dma_start(x_three[0:F, par, s * GW:s * GW + w],
                                 found[F * s:F * s + F, par, 0:w]).then_inc(flat_in[par], 16)
                sp.wait_ge(flat_in[par], dma_total(chunk, par, n_flat))
                for copy in range(1, SETS):
                    sp.dma_start(x_three[F * copy:F * copy + F, par, :],
                                 x_three[0:F, par, :]).then_inc(three_in[par], 16)

            lay_out(0, 0)
            lay_out(1, 1)
            with sp.Fori(0, CHUNKS - 3, 2) as j:
                for par in (0, 1):
                    if par == 0:
                        sp.wait_ge(mult_done, len(KINDS0) + j * STEP)
                    else:
                        sp.wait_ge(mult_done, 2 * len(KINDS0) + j * STEP)
                    lay_out(j + 2 + par, par)
            sp.wait_ge(y_ready, 1)
            sp.dma_start(out, y_sb[:, :]).then_inc(out_done, 16)
            sp.wait_ge(out_done, 16)

        @block.gpsimd
        def _(pool):
            def place_rows(chunk, par):
                nc.gpsimd.tensor_copy(rows_now[:, par, :],
                                      rows_sb[:, bass.ds(chunk * SLOTS, SLOTS)]).then_inc(rows_placed, 1)
                pool.wait_ge(rows_placed, chunk + 1)
                pool.nop(nofuse=True)

            def gather(par, slots):
                for s in slots:
                    pool.indirect_dma_start(
                        out=found[:, par, s * D:s * D + D], out_offset=None, in_=table,
                        in_offset=bass.IndirectOffsetOnAxis(ap=rows_now[:, par, s:s + 1], axis=0)
                    ).then_inc(gathered[par], 16)

            def low_part(spot):
                r, n = spot.rows, len(spot.tiles)
                pool.wait_ge(hi_done, spot.count("VP"))
                nc.gpsimd.tensor_tensor(z_lo[0:r, spot.ring, 0:n], z[0:r, spot.ring, 0:n],
                                        z_hi[0:r, spot.ring, 0:n], ALU.subtract).then_inc(lo_done["P"], 1)

            pool.wait_ge(rows_ready, 1)
            place_rows(0, 0)
            gather(0, range(SLOTS))
            place_rows(1, 1)
            gather(1, range(SLOTS))
            pool.wait_ge(flat_in[0], dma_total(0, 0, n_flat))
            place_rows(2, 0)
            gather(0, range(SLOTS))
            with pool.Fori(0, CHUNKS - 5, 2) as j:
                for n, spot in enumerate(body(j)):
                    at, nxt = n % STEP, j + n // STEP + 3
                    par = 1 - n // STEP
                    if spot.kind == "P":
                        low_part(spot)
                    if at == 0:
                        pool.wait_ge(flat_in[par], dma_total(nxt - 2, par, n_flat))
                        place_rows(nxt, par)
                    gather(par, [s for s in range(SLOTS) if GATHER_AT[s] == at])
            for n, spot in enumerate(body(CHUNKS - 4) + tail()):
                if spot.kind == "P":
                    low_part(spot)
                if n == 0:
                    pool.wait_ge(flat_in[1], dma_total(CHUNKS - 3, 1, n_flat))
                    place_rows(CHUNKS - 1, 1)
                    gather(1, range(SLOTS))

        @block.scalar
        def _(act):
            act.dma_start(w_sum[0:GP, 0:T0, :], w0a).then_inc(w0_in, 16)
            act.dma_start(w0b_sb[:, :, :], w0b).then_inc(w0_in, 16)
            act.wait_ge(select_in_done, 16)
            nc.scalar.activation(select_sb[:, :, :].rearrange("p t m -> p (t m)"), select_in,
                                 ACT.Copy).then_inc(select_ready, 1)
            act.wait_ge(wsum_ready, 1)
            nc.scalar.activation(w_hi[0:GP, 0:T0, :], w_sum[0:GP, 0:T0, :], ACT.Copy).then_inc(whi_ready, 1)
            act.wait_ge(w1_in, 16)
            nc.scalar.activation(w_hi[:, T0:, :], w_sum[:, T0:, :], ACT.Copy).then_inc(whi_ready, 1)

            def x_hi(chunk, par):
                act.wait_ge(flat_in[par], dma_total(chunk, par, n_flat))
                nc.scalar.activation(x_parts[0:F, columns(chunk)], x_three[0:F, par, :],
                                     ACT.Copy).then_inc(x_hi_done, 1)

            def high_part(spot):
                act.wait_ge(mult_done, spot.count())
                r, n = spot.rows, len(spot.tiles)
                nc.scalar.activation(z_hi[0:r, spot.ring, 0:n], z[0:r, spot.ring, 0:n],
                                     ACT.Copy).then_inc(hi_done, 1)

            def evict0(chunk, par, groups_done, reduced_before):
                act.wait_ge(contracted, groups_done)
                nc.scalar.activation(h[0:HALF, par, :], acc0[0:HALF, :], ACT.Relu).then_inc(h_ready, 1)
                nc.scalar.activation(h[HALF:P, par, :], acc0[0:HALF, :], ACT.Relu).then_inc(h_ready, 1)
                if reduced_before is not None:
                    act.wait_ge(reduced, reduced_before)
                nc.scalar.activation(direct[:, :], acc0[HALF:P, :], ACT.Relu).then_inc(evicted, 1)

            def evict1(j, groups_done):
                act.wait_ge(contracted, groups_done)
                act.wait_ge(reduced, 2 * j + 1)
                nc.scalar.activation(cur1[:, :], acc1[:, :], ACT.Relu).then_inc(evicted, 1)

            def run(spots):
                for n, spot in enumerate(spots):
                    if spot.kind in "VP":
                        high_part(spot)
                    if spot.layer == 0:
                        continue
                    before = spot.count() - 1 - spot.k
                    if spot.k == HI_AT and not spot.late:
                        x_hi(spot.chunk + 2, spot.parity)
                    if spot.k == EVICT1_AT and not spot.first:
                        evict1(spot.chunk - 1, before if spot.final else before - len(KINDS0))
                    if spot.k == EVICT0_AT and not spot.final:
                        evict0(spot.chunk + 1, 1 - spot.parity, before, 2 * spot.chunk + 1)

            act.wait_ge(gap_cleared, 1)
            x_hi(0, 0)
            lead = len(prologue())
            run(head()[:2])
            x_hi(1, 1)
            run(head()[2:lead])
            evict0(0, 0, len(KINDS0), None)
            run(head()[lead:])
            with act.Fori(0, CHUNKS - 3, 2) as j:
                run(turn(j))
            run(rest())
            evict1(CHUNKS - 1, tail()[-1].count())

            act.wait_ge(mlp_in, 16 * 8)
            for m in range(M1 // P):
                act.wait_ge(hid1_done, m + 1)
                nc.scalar.activation(hid1[m], hid1_acc[m], ACT.Relu, bias=bt1_sb[:, m:m + 1]).then_inc(hid1_relu, 1)
            for m in range(M2 // P):
                act.wait_ge(hid2_done, m + 1)
                nc.scalar.activation(hid2[m], hid2_acc[m], ACT.Relu, bias=bt2_sb[:, m:m + 1]).then_inc(hid2_relu, 1)
            act.wait_ge(y_done, 1)
            nc.scalar.activation(y_sb[:, :], acc0[0:1, :], ACT.Copy).then_inc(y_ready, 1)

        @block.vector
        def _(dve):
            def x_lo(chunk, par):
                dve.wait_ge(x_hi_done, chunk + 1)
                nc.vector.tensor_tensor(x_parts[LO:XR, columns(chunk)], x_three[0:F, par, :],
                                        x_parts[0:F, columns(chunk)], ALU.subtract).then_inc(x_lo_done, 1)

            def multiply(spot, reuses=True):
                r, n = spot.rows, len(spot.tiles)
                if spot.k == 0 and spot.layer == 0:
                    dve.wait_ge(three_in[spot.parity], dma_total(spot.chunk, spot.parity, n_three))
                if spot.k == 0 and spot.layer == 1:
                    dve.wait_ge(h_ready, 2 * spot.chunk + 2)
                if reuses:
                    dve.wait_ge(contracted, spot.count() - RING)
                dve.wait_ge(spread_done, spot.count())
                with_ = x_three[:, spot.parity, :] if spot.layer == 0 else h[:, spot.parity, :]
                nc.vector.tensor_tensor(z[0:r, spot.ring, 0:n], spread[0:r, spot.pair, 0:n],
                                        spread_rows(with_, n), ALU.mult).then_inc(mult_done, 1)

            def spread_rows(ap, n):
                return ap.unsqueeze(1).to_broadcast([ap.shape[0], n, N])

            def low_part(spot):
                r, n = spot.rows, len(spot.tiles)
                dve.wait_ge(hi_done, spot.count("VP"))
                nc.vector.tensor_tensor(z_lo[0:r, spot.ring, 0:n], z[0:r, spot.ring, 0:n],
                                        z_hi[0:r, spot.ring, 0:n], ALU.subtract).then_inc(lo_done["V"], 1)

            def reduce0(chunk, item):
                dve.wait_ge(evicted, item)
                nc.vector.tensor_reduce(feat_b[0:HALF, bass.ds(chunk * CB, CB)],
                                        direct[:, :].rearrange("p (b d) -> p b d", d=D), AX.X,
                                        ALU.add).then_inc(reduced, 1)

            def reduce1(chunk, item):
                dve.wait_ge(evicted, item)
                nc.vector.tensor_reduce(feat_a[:, bass.ds(chunk * CB, CB)],
                                        cur1[:, :].rearrange("p (b d) -> p b d", d=D), AX.X,
                                        ALU.add).then_inc(reduced, 1)

            dve.wait_ge(ids_in, 32)
            nc.vector.tensor_scalar(rows_sb[:, :], ids_sb[:, :], base_sb[:, 0:1], None,
                                    ALU.add).then_inc(rows_ready, 1)
            nc.vector.memset(x_parts[LO // 2:LO, :].bitcast(F32), 0.0).then_inc(gap_cleared, 1)
            dve.wait_ge(w0_in, 32)
            nc.vector.tensor_tensor(w_sum[0:GP, 0:T0, :], w_sum[0:GP, 0:T0, :], w0b_sb[:, :, :],
                                    ALU.add).then_inc(wsum_ready, 1)
            for n, (r, t) in enumerate(((GP, slice(0, T0)), (P, slice(T0, TILES)))):
                dve.wait_ge(whi_ready, n + 1)
                nc.vector.tensor_tensor(w_lo[0:r, t, :], w_sum[0:r, t, :], w_hi[0:r, t, :],
                                        ALU.subtract).then_inc(wlo_ready, 1)

            def run(spots, after, n_before=None):
                for n, spot in enumerate(spots):
                    if n_before is not None and n_before + n + MULT_AHEAD == len(KINDS0):
                        x_lo(1, 1)
                    if n + MULT_AHEAD < len(spots + after):
                        multiply((spots + after)[n + MULT_AHEAD],
                                 reuses=n_before is None or n_before + n + MULT_AHEAD >= RING)
                    if spot.kind == "V":
                        low_part(spot)
                    if n_before is not None and n_before + n == len(prologue()):
                        reduce0(0, 1)
                    if spot.layer == 0:
                        continue
                    if spot.k == REDUCE1_AT and not spot.first:
                        reduce1(spot.chunk - 1, 2 * spot.chunk + 1)
                    if spot.k == REDUCE0_AT and not spot.final:
                        reduce0(spot.chunk + 1, 2 * spot.chunk + 2)
                    if spot.k == LO_AT and not spot.late:
                        x_lo(spot.chunk + 2, spot.parity)

            x_lo(0, 0)
            for n, spot in enumerate(head()[:MULT_AHEAD]):
                multiply(spot, reuses=False)
            run(head(), turn(0)[:MULT_AHEAD], 0)
            with dve.Fori(0, CHUNKS - 3, 2) as j:
                run(turn(j), turn(j + 2)[:MULT_AHEAD])
            run(rest(), [])
            reduce1(CHUNKS - 1, 2 * CHUNKS)

        @block.tensor
        def _(pe):
            def spread_x(spot, reuses=True):
                if spot.k == 0 and spot.layer == 0:
                    pe.wait_ge(x_lo_done, spot.chunk + 1)
                if reuses:
                    pe.wait_ge(mult_done, spot.count() - PAIRS)
                for a, t in enumerate(spot.tiles):
                    last = nc.tensor.matmul(spread[0:spot.rows, spot.pair, a, :], select_sb[:, t, 0:spot.rows],
                                            x_parts[:, columns(spot.chunk)], start=True, stop=True)
                last.then_inc(spread_done, 1)

            def contract(spot, reuses=True):
                r = spot.rows
                acc = acc1[:, :] if spot.layer else acc0[:, :]
                if spot.k == 0 and spot.layer == 0 and not reuses and spot.parity:
                    pe.wait_ge(evicted, 1)
                elif spot.k == 0 and reuses:
                    pe.wait_ge(evicted, 2 * spot.chunk + 1 if spot.layer else 2 * spot.chunk - 2)
                if spot.kind == "W":
                    pe.wait_ge(mult_done, spot.count())
                    passes = [(w_sum, z, a) for a in range(len(spot.tiles))]
                else:
                    pe.wait_ge(hi_done, spot.count("VP"))
                    passes = [(w, z_hi, a) for a in range(len(spot.tiles)) for w in (w_hi, w_lo)]
                    passes += [(w_hi, z_lo, a) for a in range(len(spot.tiles))]
                for n, (w, of, a) in enumerate(passes):
                    if of is z_lo and a == 0:
                        pe.wait_ge(lo_done[spot.kind], spot.count(spot.kind))
                    last = nc.tensor.matmul(acc, w[0:r, spot.tiles[a], :], of[0:r, spot.ring, a, :],
                                            start=(spot.k == 0 and n == 0),
                                            stop=(spot.last and n == len(passes) - 1))
                last.then_inc(contracted, 1)

            pe.wait_ge(select_ready, 1)
            first, start = prologue(), body(0)
            for n, spot in enumerate(first[:SPREAD_AHEAD]):
                spread_x(spot, reuses=n >= PAIRS)
            pe.wait_ge(wlo_ready, 2)
            for n, spot in enumerate(first):
                spread_x((first + start)[n + SPREAD_AHEAD])
                contract(spot, reuses=False)
            with pe.Fori(0, CHUNKS - 3, 2) as j:
                spots, after = body(j), body(j + 2)
                for n, spot in enumerate(spots):
                    spread_x((spots + after)[n + SPREAD_AHEAD])
                    contract(spot)
            last = tail()
            for n, spot in enumerate(last):
                if n + SPREAD_AHEAD < len(last):
                    spread_x(last[n + SPREAD_AHEAD])
                contract(spot)

            pe.wait_ge(mlp_in, 16 * 8)
            pe.wait_ge(reduced, 2 * CHUNKS)
            for m in range(M1 // P):
                cols = slice(m * P, m * P + P)
                nc.tensor.matmul(hid1_acc[m], wt1b_sb[:, cols], feat_b[:, :], start=True, stop=False)
                nc.tensor.matmul(hid1_acc[m], wt1a_sb[:, cols], feat_a[:, :], start=False,
                                 stop=True).then_inc(hid1_done, 1)
            for m in range(M2 // P):
                for k in range(M1 // P):
                    if m == 0:
                        pe.wait_ge(hid1_relu, k + 1)
                    last = nc.tensor.matmul(hid2_acc[m], wt2_sb[:, k, m * P:m * P + P], hid1[k],
                                            start=(k == 0), stop=(k == M1 // P - 1))
                last.then_inc(hid2_done, 1)
            for k in range(M2 // P):
                pe.wait_ge(hid2_relu, k + 1)
                last = nc.tensor.matmul(acc0[0:1, :], wt3_sb[:, k:k + 1], hid2[k],
                                        start=(k == 0), stop=(k == M2 // P - 1))
            last.then_inc(y_done, 1)


def layout(inputs):
    ids = np.ascontiguousarray(inputs["ids"]).astype(np.int32)
    tables = [np.ascontiguousarray(inputs[f"tbl_{f}"]) for f in range(F)]
    by_set = np.zeros((SETS, F, CHUNKS, SLOTS), np.int32)
    for s in range(SETS):
        w = SET_ROWS[s]
        rows = ids.reshape(CHUNKS, CB, F)[:, s * SLOTS:s * SLOTS + w]
        by_set[s, :, :, 0:w] = rows.transpose(2, 0, 1)
    starts = np.cumsum([0] + [t.shape[0] for t in tables])[:F].astype(np.float32)

    w0 = np.asarray(inputs["L0_rec_W0"]).reshape(F, F, P)
    w0a, w0b = np.zeros((2, GP, T0, P), np.float32)
    select = np.zeros((XR, TILES, P), np.float32)
    i = np.arange(F)
    for o in range(OFFSETS):
        t, a = divmod(o, SETS)
        j = (i + o) % F
        w0a[F * a + i, t] = w0[i, j]
        if o:
            w0b[F * a + i, t] = w0[j, i]
        for part in (0, LO):
            select[part + j, t, F * a + i] = 1.0
    w1 = np.zeros((T1 * 2, HALF, P), np.float32)
    w1[0:F] = np.asarray(inputs["L0_rec_W1"]).reshape(F, HALF, P)
    for n in range(F):
        for part in (0, LO):
            select[part + n, T0 + n // 2, HALF * (n % 2):HALF * (n % 2) + HALF] = 1.0
    return {
        "ids": by_set.reshape(GP, CHUNKS * SLOTS),
        "base": np.tile(starts, SETS).reshape(GP, 1),
        "table": np.concatenate(tables),
        "select": select.reshape(XR, TILES * P),
        "w0a": w0a,
        "w0b": w0b,
        "w1": np.ascontiguousarray(w1.reshape(T1, P, P).transpose(1, 0, 2)),
        "wt1": np.asarray(inputs["W_top1"]),
        "bt1": np.ascontiguousarray(np.asarray(inputs["b_top1"]).reshape(M1 // P, P).T),
        "wt2": np.ascontiguousarray(np.asarray(inputs["W_top2"]).reshape(M1 // P, P, M2).transpose(1, 0, 2)),
        "bt2": np.ascontiguousarray(np.asarray(inputs["b_top2"]).reshape(M2 // P, P).T),
        "wt3": np.ascontiguousarray(np.asarray(inputs["W_top3"]).reshape(M2 // P, P).T),
        "dense": np.ascontiguousarray(np.asarray(inputs["dense_ctx"]).T),
    }


def kernel(**inputs):
    import concourse.bacc as bacc
    from concourse.bass_utils import run_bass_kernel_spmd

    nc = bacc.Bacc("TRN2", target_bir_lowering=False, num_devices=1)
    arrays, args = {}, []
    for name, a in layout(inputs).items():
        arrays[f"in_{name}_dram"] = a
        args.append(nc.dram_tensor(f"in_{name}_dram", a.shape, mybir.dt.from_np(a.dtype), kind="ExternalInput").ap())
    args.append(nc.dram_tensor("out_0_dram", (1, B), F32, kind="ExternalOutput").ap())
    build(nc, *args)
    got = run_bass_kernel_spmd(nc, [arrays], core_ids=[0]).results[0]["out_0_dram"]
    return got.reshape(B, 1)
```

```python
from contextlib import ExitStack

import numpy as np

import concourse.bass as bass
from concourse import mybir

ALU = mybir.AluOpType
ACT = mybir.ActivationFunctionType
AX = mybir.AxisListType
F32 = mybir.dt.float32
F32R = mybir.dt.float32r
I32 = mybir.dt.int32
U32 = mybir.dt.uint32

P = 128
B = 512
F = 39
D = 16
HALF = 64
CB = 32
N = CB * D
CHUNKS = B // CB
SETS = 3
GP = SETS * F
SLOTS = -(-CB // SETS)
GW = SLOTS * D
SET_ROWS = [SLOTS, SLOTS, CB - 2 * SLOTS]
OFFSETS = F // 2 + 1
T0 = -(-OFFSETS // SETS)
T1 = -(-F // 2)
TILES = T0 + T1
LO = 64
XR = LO + F
DENSE = 16
M1, M2 = 512, 256

KINDS0 = "WWWW"
KINDS1 = "WVPWPVPVPVV"
GROUPS0 = [[t for t in (2 * g, 2 * g + 1) if t < T0] for g in range(len(KINDS0))]
GROUPS1 = [[T0 + 2 * g, T0 + 2 * g + 1] for g in range(len(KINDS1) - 2)] + [[TILES - 2], [TILES - 1]]
WIDE_AT = [0, 1, 2, 3, 4]
WIDE = len(WIDE_AT)
SPREAD_AT = [k for k in range(len(KINDS1)) if k not in WIDE_AT]
SPREAD_TILES = [t for k in SPREAD_AT for t in GROUPS1[k]]
I_PAIR = {t: n for n, t in enumerate([t for k in WIDE_AT for t in GROUPS1[k]] + SPREAD_TILES)}
STEP = len(KINDS1) + len(KINDS0)
RING = 6
PAIRS = 3
SPREAD_AHEAD = 5
GATHER_AT = [0, 1, 2, 3, 4, 6, 8, 10, 11, 12, 13]
TURN = 4
EVICT1_AT = 0
EVICT0_AT = 5
REDUCE1_AT = 2
REDUCE0_AT = 6
HI_AT = 9
LO_AT = 8
MULT_AHEAD = 2


class Spot:

    def __init__(self, layer, chunk, parity, k, index, bases, before):
        self.layer, self.chunk, self.parity, self.k = layer, chunk, parity, k
        self.kind = (KINDS0, KINDS1)[layer][k]
        self.tiles = (GROUPS0, GROUPS1)[layer][k]
        self.last = k == len((KINDS0, KINDS1)[layer]) - 1
        self.ring = index % RING
        self.pair = index % PAIRS
        self.rows = GP if layer == 0 else P
        self.first = isinstance(chunk, int) and chunk == 0
        self.late = isinstance(chunk, int) and chunk >= CHUNKS - 2
        self.final = isinstance(chunk, int) and chunk == CHUNKS - 1
        self.bases, self.upto = bases, before

    def spreads(self):
        return self.chunk * len(SPREAD_AT) + SPREAD_AT.index(self.k) + 1

    def count(self, kinds="WVP"):
        return sum(self.upto[x] for x in kinds) + sum(self.bases[x] for x in kinds)


def segment(groups, bases, start):
    seen, out = {"W": 0, "V": 0, "P": 0}, []
    for index, (layer, chunk, parity, k) in enumerate(groups, start):
        seen[(KINDS0, KINDS1)[layer][k]] += 1
        out.append(Spot(layer, chunk, parity, k, index, bases, dict(seen)))
    return out


def layer_groups(layer, chunk, parity):
    return [(layer, chunk, parity, k) for k in range(len((KINDS0, KINDS1)[layer]))]


def prologue():
    return segment(layer_groups(0, 0, 0) + layer_groups(0, 1, 1), {x: 0 for x in "WVP"}, 0)


def body(j):
    bases = {x: 2 * KINDS0.count(x) + j * (KINDS0 + KINDS1).count(x) for x in "WVP"}
    return segment(layer_groups(1, j, 0) + layer_groups(0, j + 2, 0)
                   + layer_groups(1, j + 1, 1) + layer_groups(0, j + 3, 1), bases, 2 * len(KINDS0))


def tail():
    bases = {x: 2 * KINDS0.count(x) + (CHUNKS - 2) * (KINDS0 + KINDS1).count(x) for x in "WVP"}
    return segment(layer_groups(1, CHUNKS - 2, 0) + layer_groups(1, CHUNKS - 1, 1), bases, 2 * len(KINDS0))


def head():
    return prologue() + body(0)[:TURN]


def turn(j):
    return body(j)[TURN:] + body(j + 2)[:TURN]


def rest():
    return tail()[TURN:]


def build(nc, ids, base, table, select, w0a, w0b, w1, wt1, bt1, wt2, bt2, wt3, dense, out):
    assert (2 * STEP) % RING == 0 and (2 * STEP) % PAIRS == 0
    with ExitStack() as ctx:
        def sb(name, shape, dt=F32):
            return ctx.enter_context(nc.sbuf_tensor(name, shape, dt))

        def sem(name):
            return ctx.enter_context(nc.semaphore(name))

        ids_sb = sb("ids_sb", [GP, CHUNKS * SLOTS], I32)
        base_sb = sb("base_sb", [GP, 1])
        rows_sb = sb("rows_sb", [GP, CHUNKS * SLOTS], U32)
        rows_now = sb("rows_now", [GP, 2, SLOTS], U32)
        found = sb("found", [GP, 2, GW])
        x_rows = nc.dram_tensor("x_rows", (2, 2 * F, N), F32, kind="Internal")
        x_three = sb("x_three", [GP, 2, N])
        x_turned = sb("x_turned", [GP, 2, T0, N])
        x_wide = sb("x_wide", [P, 2 * WIDE, N])
        x_parts = sb("x_parts", [XR, 2, N], F32R)
        select_sb = sb("select_sb", [XR, len(SPREAD_TILES), P], F32R)
        w_sum = sb("w_sum", [P, TILES, P])
        w_hi = sb("w_hi", [P, T1, P], F32R)
        w_lo = sb("w_lo", [P, T1, P], F32R)
        z = sb("z", [P, RING, 2, N])
        staging = z[:, :, :, :].rearrange("p r a n -> p (r a n)")
        select_in = staging[0:XR, 0:len(SPREAD_TILES) * P]
        w0b_sb = staging[0:GP, TILES * P:(TILES + T0) * P].rearrange("p (t m) -> p t m", m=P)
        z_hi = sb("z_hi", [P, RING, 2, N], F32R)
        z_lo = sb("z_lo", [P, RING, 2, N], F32R)
        h = sb("h", [P, 2, N])
        direct = sb("direct", [HALF, N])
        cur1 = sb("cur1", [P, N])
        feat_a = sb("feat_a", [P, B])
        feat_b = sb("feat_b", [HALF + DENSE, B])
        wt1a_sb = sb("wt1a_sb", [P, M1])
        wt1b_sb = sb("wt1b_sb", [HALF + DENSE, M1])
        wt2_sb = sb("wt2_sb", [P, M1 // P, M2])
        wt3_sb = sb("wt3_sb", [P, M2 // P])
        bt1_sb = sb("bt1_sb", [P, M1 // P])
        bt2_sb = sb("bt2_sb", [P, M2 // P])
        y_sb = sb("y_sb", [1, B])

        spread = ctx.enter_context(nc.psum_tensor("spread", [P, PAIRS, 2, N], F32))
        acc0 = ctx.enter_context(nc.psum_tensor("acc0", [P, N], F32))
        acc1 = ctx.enter_context(nc.psum_tensor("acc1", [P, N], F32))

        hid1 = [z[:, m // 2, m % 2, :] for m in range(M1 // P)]
        hid2 = [z[:, 2, m, :] for m in range(M2 // P)]
        hid1_acc = [spread[:, m // 2, m % 2, :] for m in range(M1 // P)]
        hid2_acc = [spread[:, 2, m, :] for m in range(M2 // P)]

        ids_in = sem("ids_in")
        select_in_done = sem("select_in_done")
        w0_in = sem("w0_in")
        w1_in = sem("w1_in")
        mlp_in = sem("mlp_in")
        rows_ready = sem("rows_ready")
        rows_placed = sem("rows_placed")
        select_ready = sem("select_ready")
        wsum_ready = sem("wsum_ready")
        whi_ready = sem("whi_ready")
        wlo_ready = sem("wlo_ready")
        wlast_ready = sem("wlast_ready")
        gathered = [sem("gathered_even"), sem("gathered_odd")]
        gap_cleared = sem("gap_cleared")
        x_hi_done = sem("x_hi_done")
        x_lo_done = sem("x_lo_done")
        rows_out = [sem("rows_out_even"), sem("rows_out_odd")]
        x_in = [sem("x_even"), sem("x_odd")]
        x_wide_in = sem("x_wide_in")
        x_rest_in = [sem("x_rest_even"), sem("x_rest_odd")]
        spread_done = sem("spread_done")
        mult_done = sem("mult_done")
        hi_done = sem("hi_done")
        lo_done = {"V": sem("lo_done_vector"), "P": sem("lo_done_pool")}
        contracted = sem("contracted")
        h_ready = sem("h_ready")
        evicted = sem("evicted")
        reduced = sem("reduced")
        hid1_done = sem("hid1_done")
        hid1_relu = sem("hid1_relu")
        hid2_done = sem("hid2_done")
        hid2_relu = sem("hid2_relu")
        y_done = sem("y_done")
        y_ready = sem("y_ready")
        out_done = sem("out_done")

        n_rows, n_x, n_rest = SETS, 3, T0 - 2

        def dma_total(chunk, parity, per_chunk):
            return 8 * per_chunk * (chunk - parity) + 16 * per_chunk

        block = ctx.enter_context(nc.Block())

        @block.sync
        def _(sp):
            sp.dma_start(ids_sb[:, :], ids).then_inc(ids_in, 16)
            sp.dma_start(select_in, select).then_inc(select_in_done, 16)
            sp.dma_start(w_sum[:, T0:, :], w1).then_inc(w1_in, 16)
            for dst, src in ((wt1a_sb[:, :], wt1[HALF:HALF + P, :]),
                             (wt1b_sb[0:HALF, :], wt1[0:HALF, :]),
                             (wt1b_sb[HALF:, :], wt1[HALF + P:, :]),
                             (wt2_sb[:, :, :], wt2), (wt3_sb[:, :], wt3), (bt1_sb[:, :], bt1),
                             (bt2_sb[:, :], bt2), (feat_b[HALF:, :], dense)):
                sp.dma_start(dst, src).then_inc(mlp_in, 16)

            def lay_out(chunk, par):
                sp.wait_ge(gathered[par], dma_total(chunk, par, SLOTS))
                for s in range(SETS):
                    w = SET_ROWS[s] * D
                    sp.dma_start(x_rows[par, :, s * GW:s * GW + w].rearrange("(c f) n -> f c n", c=2),
                                 found[F * s:F * s + F, par, 0:w].unsqueeze(1).to_broadcast([F, 2, w])
                                 ).then_inc(rows_out[par], 16)
                sp.wait_ge(rows_out[par], dma_total(chunk, par, n_rows))
                def rows(first, step):
                    start = x_rows[par, first, 0:1]
                    return bass.AP(start.tensor, start.offset, [[step * N, SETS], [N, F], [1, N]])

                sp.dma_start(x_three[:, par, :], rows(0, 0)).then_inc(x_in[par], 16)
                for t in range(T0):
                    sp.dma_start(x_turned[:, par, t, :], rows(SETS * t, 1)
                                 ).then_inc(x_in[par] if t < 2 else x_rest_in[par], 16)

            def widen(par, halves=(0, 1)):
                for a in halves:
                    start = x_rows[par, a, 0:1]
                    sp.dma_start(x_wide[HALF * a:HALF * a + HALF, :, :],
                                 bass.AP(start.tensor, start.offset, [[0, HALF], [2 * N, 2 * WIDE], [1, N]])
                                 ).then_inc(x_wide_in, 16)

            lay_out(0, 0)
            widen(0, [0])
            lay_out(1, 1)
            widen(0, [1])
            with sp.Fori(0, CHUNKS - 3, 2) as j:
                for par in (0, 1):
                    sp.wait_ge(mult_done, 2 * len(KINDS0) + WIDE_AT[0] + 1 + (j + par) * STEP)
                    lay_out(j + 2 + par, par)
                    sp.wait_ge(mult_done, 2 * len(KINDS0) + WIDE_AT[-1] + 1 + (j + par) * STEP)
                    widen(1 - par)
            sp.wait_ge(mult_done, 2 * len(KINDS0) + WIDE_AT[-1] + 1 + (CHUNKS - 2) * STEP)
            widen(1)
            sp.wait_ge(y_ready, 1)
            sp.dma_start(out, y_sb[:, :]).then_inc(out_done, 16)
            sp.wait_ge(out_done, 16)

        @block.gpsimd
        def _(pool):
            def place_rows(chunk, par):
                nc.gpsimd.tensor_copy(rows_now[:, par, :],
                                      rows_sb[:, bass.ds(chunk * SLOTS, SLOTS)]).then_inc(rows_placed, 1)
                pool.wait_ge(rows_placed, chunk + 1)
                pool.nop(nofuse=True)

            def gather(par, slots):
                for s in slots:
                    pool.indirect_dma_start(
                        out=found[:, par, s * D:s * D + D], out_offset=None, in_=table,
                        in_offset=bass.IndirectOffsetOnAxis(ap=rows_now[:, par, s:s + 1], axis=0)
                    ).then_inc(gathered[par], 16)

            def low_part(spot):
                r, n = spot.rows, len(spot.tiles)
                pool.wait_ge(hi_done, spot.count("VP"))
                nc.gpsimd.tensor_tensor(z_lo[0:r, spot.ring, 0:n], z[0:r, spot.ring, 0:n],
                                        z_hi[0:r, spot.ring, 0:n], ALU.subtract).then_inc(lo_done["P"], 1)

            pool.wait_ge(rows_ready, 1)
            place_rows(0, 0)
            gather(0, range(SLOTS))
            place_rows(1, 1)
            gather(1, range(SLOTS))
            pool.wait_ge(rows_out[0], dma_total(0, 0, n_rows))
            place_rows(2, 0)
            gather(0, range(SLOTS))
            with pool.Fori(0, CHUNKS - 5, 2) as j:
                for n, spot in enumerate(body(j)):
                    at, nxt = n % STEP, j + n // STEP + 3
                    par = 1 - n // STEP
                    if spot.kind == "P":
                        low_part(spot)
                    if at == 0:
                        pool.wait_ge(rows_out[par], dma_total(nxt - 2, par, n_rows))
                        place_rows(nxt, par)
                    gather(par, [s for s in range(SLOTS) if GATHER_AT[s] == at])
            for n, spot in enumerate(body(CHUNKS - 4) + tail()):
                if spot.kind == "P":
                    low_part(spot)
                if n == 0:
                    pool.wait_ge(rows_out[1], dma_total(CHUNKS - 3, 1, n_rows))
                    place_rows(CHUNKS - 1, 1)
                if n < STEP:
                    gather(1, [s for s in range(SLOTS) if GATHER_AT[s] == n])

        @block.scalar
        def _(act):
            act.dma_start(base_sb[:, :], base).then_inc(ids_in, 16)
            act.dma_start(w_sum[0:GP, 0:T0, :], w0a).then_inc(w0_in, 16)
            act.dma_start(w0b_sb[:, :, :], w0b).then_inc(w0_in, 16)
            act.wait_ge(select_in_done, 16)
            nc.scalar.activation(select_sb[:, :, :].rearrange("p t m -> p (t m)"), select_in,
                                 ACT.Copy).then_inc(select_ready, 1)
            act.wait_ge(w1_in, 16)
            nc.scalar.activation(w_hi[:, :, :], w_sum[:, T0:, :], ACT.Copy).then_inc(whi_ready, 1)

            def x_hi(chunk, par):
                act.wait_ge(x_in[par], dma_total(chunk, par, n_x))
                if not isinstance(chunk, int) or chunk >= 2:
                    act.wait_ge(spread_done, (chunk - 1) * len(SPREAD_AT))
                nc.scalar.activation(x_parts[0:F, par, :], x_three[0:F, par, :],
                                     ACT.Copy).then_inc(x_hi_done, 1)

            def high_part(spot):
                act.wait_ge(mult_done, spot.count())
                r, n = spot.rows, len(spot.tiles)
                nc.scalar.activation(z_hi[0:r, spot.ring, 0:n], z[0:r, spot.ring, 0:n],
                                     ACT.Copy).then_inc(hi_done, 1)

            def evict0(chunk, par, groups_done, reduced_before):
                act.wait_ge(contracted, groups_done)
                nc.scalar.activation(h[0:HALF, par, :], acc0[0:HALF, :], ACT.Relu).then_inc(h_ready, 1)
                nc.scalar.activation(h[HALF:P, par, :], acc0[0:HALF, :], ACT.Relu).then_inc(h_ready, 1)
                if reduced_before is not None:
                    act.wait_ge(reduced, reduced_before)
                nc.scalar.activation(direct[:, :], acc0[HALF:P, :], ACT.Relu).then_inc(evicted, 1)

            def evict1(j, groups_done):
                act.wait_ge(contracted, groups_done)
                act.wait_ge(reduced, 2 * j + 1)
                nc.scalar.activation(cur1[:, :], acc1[:, :], ACT.Relu).then_inc(evicted, 1)

            def run(spots):
                for n, spot in enumerate(spots):
                    if spot.kind in "VP":
                        high_part(spot)
                    if spot.layer == 0:
                        continue
                    before = spot.count() - 1 - spot.k
                    if spot.k == HI_AT and not spot.late:
                        x_hi(spot.chunk + 2, spot.parity)
                    if spot.k == EVICT1_AT and not spot.first:
                        evict1(spot.chunk - 1, before if spot.final else before - len(KINDS0))
                    if spot.k == EVICT0_AT and not spot.final:
                        evict0(spot.chunk + 1, 1 - spot.parity, before, 2 * spot.chunk + 1)

            act.wait_ge(gap_cleared, 1)
            x_hi(0, 0)
            lead = len(prologue())
            run(head()[:2])
            x_hi(1, 1)
            run(head()[2:lead])
            evict0(0, 0, len(KINDS0), None)
            run(head()[lead:])
            with act.Fori(0, CHUNKS - 3, 2) as j:
                run(turn(j))
            run(rest())
            evict1(CHUNKS - 1, tail()[-1].count())

            act.wait_ge(mlp_in, 16 * 8)
            for m in range(M1 // P):
                act.wait_ge(hid1_done, M1 // P + m + 1)
                nc.scalar.activation(hid1[m], hid1_acc[m], ACT.Relu, bias=bt1_sb[:, m:m + 1]).then_inc(hid1_relu, 1)
            for m in range(M2 // P):
                act.wait_ge(hid2_done, m + 1)
                nc.scalar.activation(hid2[m], hid2_acc[m], ACT.Relu, bias=bt2_sb[:, m:m + 1]).then_inc(hid2_relu, 1)
            act.wait_ge(y_done, 1)
            nc.scalar.activation(y_sb[:, :], acc0[0:1, :], ACT.Copy).then_inc(y_ready, 1)

        @block.vector
        def _(dve):
            def x_lo(chunk, par):
                dve.wait_ge(x_hi_done, chunk + 1)
                nc.vector.tensor_tensor(x_parts[LO:XR, par, :], x_three[0:F, par, :],
                                        x_parts[0:F, par, :], ALU.subtract).then_inc(x_lo_done, 1)

            def multiply(spot, reuses=True):
                r, n = spot.rows, len(spot.tiles)
                if spot.k == 0 and spot.layer == 0:
                    dve.wait_ge(x_in[spot.parity], dma_total(spot.chunk, spot.parity, n_x))
                if spot.k == 1 and spot.layer == 0:
                    dve.wait_ge(x_rest_in[spot.parity], dma_total(spot.chunk, spot.parity, n_rest))
                if spot.k == 0 and spot.layer == 1:
                    dve.wait_ge(h_ready, 2 * spot.chunk + 2)
                    dve.wait_ge(x_wide_in, 32 * spot.chunk + 32)
                if reuses:
                    dve.wait_ge(contracted, spot.count() - RING)
                if spot.layer == 0:
                    of = x_turned[:, spot.parity, spot.tiles[0]:spot.tiles[-1] + 1, :]
                    by = x_three[:, spot.parity, :]
                elif spot.k in WIDE_AT:
                    at = 2 * WIDE_AT.index(spot.k)
                    of, by = x_wide[:, at:at + n, :], h[:, spot.parity, :]
                else:
                    dve.wait_ge(spread_done, spot.spreads())
                    of, by = spread[:, spot.pair, 0:n], h[:, spot.parity, :]
                nc.vector.tensor_tensor(z[0:r, spot.ring, 0:n], of, spread_rows(by, n),
                                        ALU.mult).then_inc(mult_done, 1)

            def spread_rows(ap, n):
                return ap.unsqueeze(1).to_broadcast([ap.shape[0], n, N])

            def low_part(spot):
                r, n = spot.rows, len(spot.tiles)
                dve.wait_ge(hi_done, spot.count("VP"))
                nc.vector.tensor_tensor(z_lo[0:r, spot.ring, 0:n], z[0:r, spot.ring, 0:n],
                                        z_hi[0:r, spot.ring, 0:n], ALU.subtract).then_inc(lo_done["V"], 1)

            def reduce0(chunk, item):
                dve.wait_ge(evicted, item)
                nc.vector.tensor_reduce(feat_b[0:HALF, bass.ds(chunk * CB, CB)],
                                        direct[:, :].rearrange("p (b d) -> p b d", d=D), AX.X,
                                        ALU.add).then_inc(reduced, 1)

            def reduce1(chunk, item):
                dve.wait_ge(evicted, item)
                nc.vector.tensor_reduce(feat_a[:, bass.ds(chunk * CB, CB)],
                                        cur1[:, :].rearrange("p (b d) -> p b d", d=D), AX.X,
                                        ALU.add).then_inc(reduced, 1)

            dve.wait_ge(ids_in, 32)
            nc.vector.tensor_scalar(rows_sb[:, :], ids_sb[:, :], base_sb[:, 0:1], None,
                                    ALU.add).then_inc(rows_ready, 1)
            nc.vector.memset(x_parts[LO // 2:LO, :, :].bitcast(F32), 0.0).then_inc(gap_cleared, 1)
            dve.wait_ge(w0_in, 32)
            nc.vector.tensor_tensor(w_sum[0:GP, 0:T0, :], w_sum[0:GP, 0:T0, :], w0b_sb[:, :, :],
                                    ALU.add).then_inc(wsum_ready, 1)
            dve.wait_ge(whi_ready, 1)
            nc.vector.tensor_tensor(w_lo[:, :, :], w_sum[:, T0:, :], w_hi[:, :, :],
                                    ALU.subtract).then_inc(wlo_ready, 1)
            dve.wait_ge(wlo_ready, 1)
            nc.vector.tensor_copy(w_hi[HALF:P, T1 - 1, :], w_lo[HALF:P, T1 - 1, :]).then_inc(wlast_ready, 1)

            def run(spots, after, n_before=None):
                for n, spot in enumerate(spots):
                    if n_before is not None and n_before + n + MULT_AHEAD == len(KINDS0):
                        x_lo(1, 1)
                    if n + MULT_AHEAD < len(spots + after):
                        multiply((spots + after)[n + MULT_AHEAD],
                                 reuses=n_before is None or n_before + n + MULT_AHEAD >= RING)
                    if spot.kind == "V":
                        low_part(spot)
                    if n_before is not None and n_before + n == len(prologue()):
                        reduce0(0, 1)
                    if spot.layer == 0:
                        continue
                    if spot.k == REDUCE1_AT and not spot.first:
                        reduce1(spot.chunk - 1, 2 * spot.chunk + 1)
                    if spot.k == REDUCE0_AT and not spot.final:
                        reduce0(spot.chunk + 1, 2 * spot.chunk + 2)
                    if spot.k == LO_AT and not spot.late:
                        x_lo(spot.chunk + 2, spot.parity)

            x_lo(0, 0)
            for n, spot in enumerate(head()[:MULT_AHEAD]):
                multiply(spot, reuses=False)
            run(head(), turn(0)[:MULT_AHEAD], 0)
            with dve.Fori(0, CHUNKS - 3, 2) as j:
                run(turn(j), turn(j + 2)[:MULT_AHEAD])
            run(rest(), [])
            reduce1(CHUNKS - 1, 2 * CHUNKS)

        @block.tensor
        def _(pe):
            def spread_x(spot, reuses=True):
                if spot.layer == 0 or spot.k in WIDE_AT:
                    return
                if spot.k == SPREAD_AT[0]:
                    pe.wait_ge(x_lo_done, spot.chunk + 1)
                if reuses:
                    pe.wait_ge(mult_done, spot.count() - PAIRS)
                for a, t in enumerate(spot.tiles):
                    last = nc.tensor.matmul(spread[:, spot.pair, a, :], select_sb[:, SPREAD_TILES.index(t), :],
                                            x_parts[:, spot.parity, :], start=True, stop=True)
                last.then_inc(spread_done, 1)

            def contract(spot, reuses=True):
                r = spot.rows
                acc = acc1[:, :] if spot.layer else acc0[:, :]
                if spot.k == 0 and spot.layer == 0 and not reuses and spot.parity:
                    pe.wait_ge(evicted, 1)
                elif spot.k == 0 and reuses:
                    pe.wait_ge(evicted, 2 * spot.chunk + 1 if spot.layer else 2 * spot.chunk - 2)
                if spot.kind == "W":
                    pe.wait_ge(mult_done, spot.count())
                    passes = [(w_sum, t, z, a) for a, t in enumerate(spot.tiles)]
                elif spot.tiles[0] == TILES - 1:
                    pe.wait_ge(hi_done, spot.count("VP"))
                    passes = [(w_hi, T1 - 1, z_hi, 0), (w_hi, T1 - 1, z_lo, 0)]
                else:
                    pe.wait_ge(hi_done, spot.count("VP"))
                    passes = [(w, t - T0, z_hi, a) for a, t in enumerate(spot.tiles) for w in (w_hi, w_lo)]
                    passes += [(w_hi, t - T0, z_lo, a) for a, t in enumerate(spot.tiles)]
                for n, (w, t, of, a) in enumerate(passes):
                    if of is z_lo and a == 0:
                        pe.wait_ge(lo_done[spot.kind], spot.count(spot.kind))
                    last = nc.tensor.matmul(acc, w[0:r, t, :], of[0:r, spot.ring, a, :],
                                            start=(spot.k == 0 and n == 0),
                                            stop=(spot.last and n == len(passes) - 1))
                last.then_inc(contracted, 1)

            pe.wait_ge(select_ready, 1)
            first, start = prologue(), body(0)
            for n, spot in enumerate(first[:SPREAD_AHEAD]):
                spread_x(spot, reuses=n >= PAIRS)
            pe.wait_ge(wsum_ready, 1)
            pe.wait_ge(wlast_ready, 1)
            for n, spot in enumerate(first):
                spread_x((first + start)[n + SPREAD_AHEAD])
                contract(spot, reuses=False)
            with pe.Fori(0, CHUNKS - 3, 2) as j:
                spots, after = body(j), body(j + 2)
                for n, spot in enumerate(spots):
                    spread_x((spots + after)[n + SPREAD_AHEAD])
                    contract(spot)
            last = tail()
            for n, spot in enumerate(last):
                if n + SPREAD_AHEAD < len(last):
                    spread_x(last[n + SPREAD_AHEAD])
                contract(spot)

            pe.wait_ge(mlp_in, 16 * 8)
            early = B - CB
            for batch, so_far in ((slice(0, early), 2 * CHUNKS - 1), (slice(early, B), 2 * CHUNKS)):
                pe.wait_ge(reduced, so_far)
                for m in range(M1 // P):
                    cols = slice(m * P, m * P + P)
                    nc.tensor.matmul(hid1_acc[m][:, batch], wt1b_sb[:, cols], feat_b[:, batch],
                                     start=True, stop=False)
                    last = nc.tensor.matmul(hid1_acc[m][:, batch], wt1a_sb[:, cols], feat_a[:, batch],
                                            start=False, stop=True)
                    last.then_inc(hid1_done, 1)
            for m in range(M2 // P):
                for k in range(M1 // P):
                    if m == 0:
                        pe.wait_ge(hid1_relu, k + 1)
                    last = nc.tensor.matmul(hid2_acc[m], wt2_sb[:, k, m * P:m * P + P], hid1[k],
                                            start=(k == 0), stop=(k == M1 // P - 1))
                last.then_inc(hid2_done, 1)
            for k in range(M2 // P):
                pe.wait_ge(hid2_relu, k + 1)
                last = nc.tensor.matmul(acc0[0:1, :], wt3_sb[:, k:k + 1], hid2[k],
                                        start=(k == 0), stop=(k == M2 // P - 1))
            last.then_inc(y_done, 1)


def layout(inputs):
    ids = np.ascontiguousarray(inputs["ids"]).astype(np.int32)
    tables = [np.ascontiguousarray(inputs[f"tbl_{f}"]) for f in range(F)]
    by_set = np.zeros((SETS, F, CHUNKS, SLOTS), np.int32)
    for s in range(SETS):
        w = SET_ROWS[s]
        rows = ids.reshape(CHUNKS, CB, F)[:, s * SLOTS:s * SLOTS + w]
        by_set[s, :, :, 0:w] = rows.transpose(2, 0, 1)
    starts = np.cumsum([0] + [t.shape[0] for t in tables])[:F].astype(np.float32)

    w0 = np.asarray(inputs["L0_rec_W0"]).reshape(F, F, P)
    w0a, w0b = np.zeros((2, GP, T0, P), np.float32)
    select = np.zeros((XR, T1, P), np.float32)
    i = np.arange(F)
    for o in range(OFFSETS):
        t, a = divmod(o, SETS)
        j = (i + o) % F
        w0a[F * a + i, t] = w0[i, j]
        if o:
            w0b[F * a + i, t] = w0[j, i]
    w1 = np.zeros((P, T1, P), np.float32)
    from_w1 = np.asarray(inputs["L0_rec_W1"]).reshape(F, HALF, P)
    for t, pair in I_PAIR.items():
        for a in range(2):
            n, rows = min(2 * pair + a, F - 1), slice(HALF * a, HALF * a + HALF)
            w1[rows, t - T0] = from_w1[n]
            for part in (0, LO):
                select[part + n, t - T0, rows] = 1.0
    select = select[:, [t - T0 for t in SPREAD_TILES]]
    return {
        "ids": by_set.reshape(GP, CHUNKS * SLOTS),
        "base": np.tile(starts, SETS).reshape(GP, 1),
        "table": np.concatenate(tables),
        "select": select.reshape(XR, len(SPREAD_TILES) * P),
        "w0a": w0a,
        "w0b": w0b,
        "w1": w1,
        "wt1": np.asarray(inputs["W_top1"]),
        "bt1": np.ascontiguousarray(np.asarray(inputs["b_top1"]).reshape(M1 // P, P).T),
        "wt2": np.ascontiguousarray(np.asarray(inputs["W_top2"]).reshape(M1 // P, P, M2).transpose(1, 0, 2)),
        "bt2": np.ascontiguousarray(np.asarray(inputs["b_top2"]).reshape(M2 // P, P).T),
        "wt3": np.ascontiguousarray(np.asarray(inputs["W_top3"]).reshape(M2 // P, P).T),
        "dense": np.ascontiguousarray(np.asarray(inputs["dense_ctx"]).T),
    }


def kernel(**inputs):
    import concourse.bacc as bacc
    from concourse.bass_utils import run_bass_kernel_spmd

    nc = bacc.Bacc("TRN2", target_bir_lowering=False, num_devices=1)
    arrays, args = {}, []
    for name, a in layout(inputs).items():
        arrays[f"in_{name}_dram"] = a
        args.append(nc.dram_tensor(f"in_{name}_dram", a.shape, mybir.dt.from_np(a.dtype), kind="ExternalInput").ap())
    args.append(nc.dram_tensor("out_0_dram", (1, B), F32, kind="ExternalOutput").ap())
    build(nc, *args)
    got = run_bass_kernel_spmd(nc, [arrays], core_ids=[0]).results[0]["out_0_dram"]
    return got.reshape(B, 1)
```
